# Optimizing a Trainium2 kernel written in Bass

```python
import numpy as np
import jax
import jax.numpy as jnp

def _softmax(x, axis=-1):
    return jax.nn.softmax(x, axis=axis)

def _gelu(x):
    return jax.nn.gelu(x, approximate=True)

def _silu(x):
    return jax.nn.silu(x)

def _sigmoid(x):
    return jax.nn.sigmoid(x)

def _layernorm(x, axis=-1, eps=1e-05):
    m = jnp.mean(x, axis=axis, keepdims=True)
    v = jnp.var(x, axis=axis, keepdims=True)
    return (x - m) / jnp.sqrt(v + eps)

def _scatter_add(tgt, idx, src, axis=0):
    return tgt.at[idx].add(src)

def _segment_sum(src, seg, n):
    return jax.ops.segment_sum(src, seg, n)
kernel_name = 'mk_flamingo_gated_d1_seqx_r8_13197e'

def setup_inputs(seed: int=0):
    np.random.seed(seed)
    _w = jnp.asarray

    def _rec_inputs():
        import jax
        import jax.numpy as jnp
        _rk = jax.random.key(seed)
        x = -0.0002928 + 1 * jax.random.normal(jax.random.fold_in(_rk, 1), (32, 128, 128), jnp.float32)
        _lenS = 128 - jax.random.randint(jax.random.fold_in(_rk, 7), (32,), 0, max(1, 128 // 4) + 1, jnp.int32)
        _lenS2 = 128 - jax.random.randint(jax.random.fold_in(_rk, 8), (32,), 0, max(1, 128 // 4) + 1, jnp.int32)
        _ctx_512P = jax.random.normal(jax.random.fold_in(_rk, 11), (32, 16, 64), jnp.float32)
        _ctx_512c = jax.random.dirichlet(jax.random.fold_in(_rk, 511), 0.3 * jnp.ones((16,), jnp.float32), (32, 128))
        _ctx_512t = jnp.einsum('bsk,bkd->bsd', _ctx_512c, _ctx_512P)
        _ctx_512t = _ctx_512t * jax.lax.rsqrt(jnp.mean(jnp.square(_ctx_512t)) + 1e-12) * 0.953939
        ctx_512 = -1.52775e-05 + 0.999936 * (_ctx_512t + 0.3 * jax.random.normal(jax.random.fold_in(_rk, 611), (32, 128, 64), jnp.float32))
        _g = jax.random.normal(jax.random.fold_in(_rk, 9001), (2, 1), jnp.float32)
        _g = jnp.sign(_g) * jnp.maximum(jnp.abs(_g), 1.0) + (_g == 0) * 1.0
        g_xattn = _g[0]
        g_ffn = _g[1]
        return (x, ctx_512, g_xattn, g_ffn)
    x, ctx_512, g_xattn, g_ffn = _rec_inputs()

    def _L0_xattn_setup():
        import jax, jax.numpy as jnp
        import numpy as np
        NUM_HEADS = 16
        HEAD_DIM = 64
        Q_DIM = 128
        KV_DIM = 64
        INNER = NUM_HEADS * HEAD_DIM
        key = jax.random.key(seed)
        ks = jax.random.split(key, 7)
        B, N, M = (32, 128, 256)
        q = jax.random.normal(ks[0], (B, N, Q_DIM), dtype=jnp.float32)
        kv = jax.random.normal(ks[1], (B, M, KV_DIM), dtype=jnp.float32)
        Wq = jax.random.normal(ks[2], (Q_DIM, INNER), dtype=jnp.float32) / np.sqrt(Q_DIM)
        Wk = jax.random.normal(ks[3], (KV_DIM, INNER), dtype=jnp.float32) / np.sqrt(KV_DIM)
        Wv = jax.random.normal(ks[4], (KV_DIM, INNER), dtype=jnp.float32) / np.sqrt(KV_DIM)
        Wo = jax.random.normal(ks[5], (INNER, Q_DIM), dtype=jnp.float32) / np.sqrt(INNER)
        bo = jax.random.normal(ks[6], (Q_DIM,), dtype=jnp.float32) * 0.01
        return {'q': q, 'kv': kv, 'Wq': Wq, 'Wk': Wk, 'Wv': Wv, 'Wo': Wo, 'bo': bo}
    _L0_xattn_all = _L0_xattn_setup()
    _L0_xattn_in = {k: v for k, v in _L0_xattn_all.items() if k in ('Wq', 'Wk', 'Wv', 'Wo', 'bo')}
    del _L0_xattn_all

    def _L0_ffn_setup():
        import jax, jax.numpy as jnp
        import numpy as np
        N_EXPERTS = 32
        TOP_K = 8
        N_GROUP = 4
        TOPK_GROUP = 2
        ROUTED_SCALING = 2.5

        def _gate(x, gate_w, gate_bias):
            T, E = (x.shape[0], gate_w.shape[0])
            logits = jnp.einsum('th,eh->te', x, gate_w)
            scores = jax.nn.sigmoid(logits)
            scores_choice = scores + gate_bias[None, :]
            grp = scores_choice.reshape(T, N_GROUP, E // N_GROUP)
            top2, _ = jax.lax.top_k(grp, 2)
            group_scores = top2.sum(-1)
            _, grp_idx = jax.lax.top_k(group_scores, TOPK_GROUP)
            group_mask = jax.nn.one_hot(grp_idx, N_GROUP, dtype=scores.dtype).sum(1)
            expert_mask = jnp.repeat(group_mask, E // N_GROUP, axis=1)
            masked = jnp.where(expert_mask > 0, scores_choice, 0.0)
            _, topk_idx = jax.lax.top_k(masked, TOP_K)
            topk_w = jnp.take_along_axis(scores, topk_idx, axis=1)
            topk_w = topk_w / (topk_w.sum(-1, keepdims=True) + 1e-20)
            topk_w = topk_w * ROUTED_SCALING
            return (topk_idx, topk_w)

        def _mlp(x, wg, wu, wd):
            return jnp.einsum('...i,hi->...h', jax.nn.silu(jnp.einsum('...h,ih->...i', x, wg)) * jnp.einsum('...h,ih->...i', x, wu), wd)
        key = jax.random.key(seed)
        ks = jax.random.split(key, 9)
        B, S, H, I = (2, 64, 128, 64)
        w = 0.02
        return {'hidden_states': jax.random.normal(ks[0], (B, S, H), jnp.float32), 'gate_w': jax.random.normal(ks[1], (N_EXPERTS, H), jnp.float32) * w, 'gate_bias': jax.random.normal(ks[2], (N_EXPERTS,), jnp.float32) * w, 'expert_gate': jax.random.normal(ks[3], (N_EXPERTS, I, H), jnp.float32) * w, 'expert_up': jax.random.normal(ks[4], (N_EXPERTS, I, H), jnp.float32) * w, 'expert_down': jax.random.normal(ks[5], (N_EXPERTS, H, I), jnp.float32) * w, 'shared_gate': jax.random.normal(ks[6], (2 * I, H), jnp.float32) * w, 'shared_up': jax.random.normal(ks[7], (2 * I, H), jnp.float32) * w, 'shared_down': jax.random.normal(ks[8], (H, 2 * I), jnp.float32) * w}
    _L0_ffn_all = _L0_ffn_setup()
    _L0_ffn_in = {k: v for k, v in _L0_ffn_all.items() if k in ('gate_w', 'gate_bias', 'expert_gate', 'expert_up', 'expert_down', 'shared_gate', 'shared_up', 'shared_down')}
    del _L0_ffn_all
    return {'x': x, 'ctx_512': ctx_512, 'g_xattn': g_xattn, 'g_ffn': g_ffn, 'L0_xattn_Wq': _L0_xattn_in['Wq'], 'L0_xattn_Wk': _L0_xattn_in['Wk'], 'L0_xattn_Wv': _L0_xattn_in['Wv'], 'L0_xattn_Wo': _L0_xattn_in['Wo'], 'L0_xattn_bo': _L0_xattn_in['bo'], 'L0_ffn_gate_w': _L0_ffn_in['gate_w'], 'L0_ffn_gate_bias': _L0_ffn_in['gate_bias'], 'L0_ffn_expert_gate': _L0_ffn_in['expert_gate'], 'L0_ffn_expert_up': _L0_ffn_in['expert_up'], 'L0_ffn_expert_down': _L0_ffn_in['expert_down'], 'L0_ffn_shared_gate': _L0_ffn_in['shared_gate'], 'L0_ffn_shared_up': _L0_ffn_in['shared_up'], 'L0_ffn_shared_down': _L0_ffn_in['shared_down']}

def reference(x, ctx_512, g_xattn, g_ffn, L0_xattn_Wq, L0_xattn_Wk, L0_xattn_Wv, L0_xattn_Wo, L0_xattn_bo, L0_ffn_gate_w, L0_ffn_gate_bias, L0_ffn_expert_gate, L0_ffn_expert_up, L0_ffn_expert_down, L0_ffn_shared_gate, L0_ffn_shared_up, L0_ffn_shared_down):
    import jax
    import jax.numpy as jnp

    def _L0_xattn_ref(q, kv, Wq, Wk, Wv, Wo, bo):
        import jax, jax.numpy as jnp
        import numpy as np
        NUM_HEADS = 16
        HEAD_DIM = 64
        Q_DIM = 128
        KV_DIM = 64
        INNER = NUM_HEADS * HEAD_DIM
        B, N, _ = q.shape
        M = kv.shape[1]
        scale = HEAD_DIM ** (-0.5)
        qh = (q @ Wq).reshape(B, N, NUM_HEADS, HEAD_DIM).transpose(0, 2, 1, 3)
        kh = (kv @ Wk).reshape(B, M, NUM_HEADS, HEAD_DIM).transpose(0, 2, 1, 3)
        vh = (kv @ Wv).reshape(B, M, NUM_HEADS, HEAD_DIM).transpose(0, 2, 1, 3)
        scores = jnp.einsum('bhnd,bhmd->bhnm', qh, kh) * scale
        attn = jax.nn.softmax(scores, axis=-1)
        out = jnp.einsum('bhnm,bhmd->bhnd', attn, vh)
        out = out.transpose(0, 2, 1, 3).reshape(B, N, INNER)
        return out @ Wo + bo

    def _L0_ffn_ref(hidden_states, gate_w, gate_bias, expert_gate, expert_up, expert_down, shared_gate, shared_up, shared_down):
        import jax, jax.numpy as jnp
        import numpy as np
        N_EXPERTS = 32
        TOP_K = 8
        N_GROUP = 4
        TOPK_GROUP = 2
        ROUTED_SCALING = 2.5

        def _gate(x, gate_w, gate_bias):
            T, E = (x.shape[0], gate_w.shape[0])
            logits = jnp.einsum('th,eh->te', x, gate_w)
            scores = jax.nn.sigmoid(logits)
            scores_choice = scores + gate_bias[None, :]
            grp = scores_choice.reshape(T, N_GROUP, E // N_GROUP)
            top2, _ = jax.lax.top_k(grp, 2)
            group_scores = top2.sum(-1)
            _, grp_idx = jax.lax.top_k(group_scores, TOPK_GROUP)
            group_mask = jax.nn.one_hot(grp_idx, N_GROUP, dtype=scores.dtype).sum(1)
            expert_mask = jnp.repeat(group_mask, E // N_GROUP, axis=1)
            masked = jnp.where(expert_mask > 0, scores_choice, 0.0)
            _, topk_idx = jax.lax.top_k(masked, TOP_K)
            topk_w = jnp.take_along_axis(scores, topk_idx, axis=1)
            topk_w = topk_w / (topk_w.sum(-1, keepdims=True) + 1e-20)
            topk_w = topk_w * ROUTED_SCALING
            return (topk_idx, topk_w)

        def _mlp(x, wg, wu, wd):
            return jnp.einsum('...i,hi->...h', jax.nn.silu(jnp.einsum('...h,ih->...i', x, wg)) * jnp.einsum('...h,ih->...i', x, wu), wd)
        orig_shape = hidden_states.shape
        H = orig_shape[-1]
        residuals = hidden_states
        x = hidden_states.reshape(-1, H)
        topk_idx, topk_w = _gate(x, gate_w, gate_bias)
        g = jnp.einsum('th,eih->eti', x, expert_gate)
        u = jnp.einsum('th,eih->eti', x, expert_up)
        outs = jnp.einsum('eti,ehi->eth', jax.nn.silu(g) * u, expert_down)
        outs_t = jnp.transpose(outs, (1, 0, 2))
        gathered = jnp.take_along_axis(outs_t, topk_idx[:, :, None], axis=1)
        final = (gathered * topk_w[:, :, None]).sum(1)
        shared = _mlp(residuals, shared_gate, shared_up, shared_down)
        return final.reshape(orig_shape) + shared
    x = x + jnp.tanh(g_xattn[0]) * _L0_xattn_ref(_layernorm(x, axis=-1), ctx_512, L0_xattn_Wq, L0_xattn_Wk, L0_xattn_Wv, L0_xattn_Wo, L0_xattn_bo)
    x = x + jnp.tanh(g_ffn[0]) * _L0_ffn_ref(_layernorm(x, axis=-1), L0_ffn_gate_w, L0_ffn_gate_bias, L0_ffn_expert_gate, L0_ffn_expert_up, L0_ffn_expert_down, L0_ffn_shared_gate, L0_ffn_shared_up, L0_ffn_shared_down)
    return x

_drawn_inputs = setup_inputs


def setup_inputs(seed=0):
    import zlib

    import numpy as np

    out = dict(_drawn_inputs(seed))
    spreads = {}
    factors = {'L0_xattn_bo': 7.577,
     'L0_ffn_gate_w': 8.0,
     'L0_ffn_gate_bias': 8.0,
     'L0_ffn_expert_gate': 8.0,
     'L0_ffn_expert_up': 8.0,
     'L0_ffn_expert_down': 8.0,
     'L0_ffn_shared_gate': 8.0,
     'L0_ffn_shared_up': 8.0,
     'L0_ffn_shared_down': 8.0}
    for name, (base, spread) in spreads.items():
        noise = np.random.default_rng([zlib.crc32(name.encode()), seed]).standard_normal(out[name].shape)
        drawn = base * np.exp(spread * noise) if base else spread * noise
        out[name] = jnp.asarray(drawn.astype(out[name].dtype))
    for name, factor in factors.items():
        out[name] = (out[name] * factor).astype(out[name].dtype)
    return out
```

```python
from contextlib import ExitStack

import concourse.bass as bass
from concourse import mybir

F32 = mybir.dt.float32
F32R = mybir.dt.float32r
BF16 = mybir.dt.bfloat16
I32 = mybir.dt.int32
ACT = mybir.ActivationFunctionType
ALU = mybir.AluOpType
AX_X = mybir.AxisListType.X

P = 128
NB = 32
D = 128
HEADS, HD, CD = 16, 64, 64
PAIRS = HEADS // 2
CB = 4
NCH = NB // CB
CT = CB * P
NE, EI = 32, 64
GROUPS, GE = 4, 8
GROUPS_TAKEN = 2
UNITS = NE // 2 + 1
FW = UNITS * P
WCOLS = 3 * FW
WSTEP = WCOLS // NB
SCALE = float(HD) ** -0.5
ROUTED_SCALING = 2.5
EPS = 1e-5
LOWEST, PICKED = -1.0e30, 3.0e38
GUESS_SCALE = 1.36 * 2.0 ** -66

NEWTON_STEPS = 3
LN_STEPS = 2 * CB + 4 + 3 * NEWTON_STEPS
ROUTE_STEPS = 53
LAG = 3
SLOTS = LAG + 1


def build(nc, x, ctx_nat, ctx_t, g_xattn, g_ffn, wq_t, wk_t, wv_t, wo, bo, router_t, router_bias, experts, out):
    with ExitStack() as stack:
        def sb(name, shape, dt=F32):
            return stack.enter_context(nc.sbuf_tensor(name, shape, dt))

        def sem(name):
            return stack.enter_context(nc.semaphore(name))

        def raw(ap):
            return ap.bitcast(F32)

        def flat(ap, n):
            return ap.rearrange({3: "p a b -> p (a b)", 4: "p a b c -> p (a b c)"}[n])

        x_sb = sb("x_sb", [P, NB, D])
        ident = sb("ident", [P, P])
        ident_bf = sb("ident_bf", [P, P], BF16)
        neg_ones = sb("neg_ones", [1, P], F32R)
        ones_row = sb("ones_row", [1, P])
        ones_col = sb("ones_col", [P, 1])
        gates = sb("gates", [P, 2])
        tanh_g = sb("tanh_g", [P, 2])
        bo_row = sb("bo_row", [1, D])
        bo_gated = sb("bo_gated", [1, D])
        area = sb("area", [P, 6, 1024])
        wq_pair, wk_diag, wv_diag, wo_pair, a_full = (
            area[:, i, :].rearrange("p (h n) -> p h n", h=PAIRS) for i in range(5))
        probs_t = area[:, 0:2, :].rearrange("p a n -> p (a n)").rearrange("p (k h n) -> p k h n", k=4, h=4)
        u_norm = area[:, 2:4, :].rearrange("p a (h q d) -> p a h q d", h=PAIRS, q=2)
        u_t = area[:, 4:6, :].rearrange("p a (h n) -> p a h n", h=PAIRS)
        silu_g, gated, hid = (area[:, i, :].rearrange("p (a n) -> p a n", a=2) for i in range(3))
        x2t, y_t, result = area[:, 3, 0:CT], area[:, 3, CT:2 * CT], area[:, 4, 0:CT]
        a_hi = sb("a_hi", [P, PAIRS, P], F32R)
        a_lo = sb("a_lo", [P, PAIRS, P], F32R)
        c_pair = sb("c_pair", [P, PAIRS, D])
        ctx_keys = sb("ctx_keys", [P, CB, CD + 1])
        ctx_raw = sb("ctx_raw", [P, CB, P])
        diag_hi = sb("diag_hi", [P, CB, 2, P], F32R)
        diag_lo = sb("diag_lo", [P, CB, 2, P], F32R)
        bn6 = sb("bn6", [P, CB, 6])
        mean_var = sb("mean_var", [P, CB, 2])
        var_eps = sb("var_eps", [P, CB])
        half_var = sb("half_var", [P, CB])
        rsqrt_bits = sb("rsqrt_bits", [P, CB])
        guess = sb("guess", [P, NEWTON_STEPS, CB])
        newton = sb("newton", [P, 2, CB])
        rstd = sb("rstd", [P, CB])
        xn = sb("xn", [P, CB, D])
        xnt_hi = sb("xnt_hi", [P, CT], F32R)
        xnt_lo = sb("xnt_lo", [P, CT], F32R)
        halves = sb("halves", [P, 2, 2 * PAIRS * 2 * P], F32R)
        g_hi, g_lo = (halves[:, i, :].rearrange("p (r h n) -> p r h n", r=2, h=PAIRS) for i in range(2))
        hid_hi, hid_lo = (halves[:, i, 0:SLOTS * CT].rearrange("p (s n) -> p s n", s=SLOTS) for i in range(2))
        row_max = sb("row_max", [P, 2, HEADS])
        max_t = sb("max_t", [HEADS, 2, P], F32R)
        max_row = sb("max_row", [1, 2, HEADS, P], F32R)
        inv_sum = sb("inv_sum", [P, 4, 4])
        w_raw = sb("w_raw", [P, 2, WSTEP])
        w_hi = sb("w_hi", [P, WCOLS], F32R)
        w_lo = sb("w_lo", [P, WCOLS], F32R)
        router_w = sb("router_w", [P, NE])
        bias_bc = sb("bias_bc", [P, NE])
        expand = sb("expand", [3 * NE, NE // 2, P], BF16)
        x2t_hi = sb("x2t_hi", [P, 2, CT], F32R)
        x2t_lo = sb("x2t_lo", [P, 2, CT], F32R)
        logits = sb("logits", [P, CB * NE])
        logits_low = sb("logits_low", [P, CB * NE])
        tanh_half = sb("tanh_half", [P, CB * NE])
        silu_low = sb("silu_low", [P, CB * NE])
        sig = sb("sig", [P, 5, CB * NE])
        score = sb("score", [P, CB, NE])
        choice = sb("choice", [P, CB, NE])
        top_in_group = sb("top_in_group", [P, CB, GROUPS, 8])
        group_score = sb("group_score", [P, CB, GROUPS + 6])
        group_top = sb("group_top", [P, CB, 8])
        group_pick = sb("group_pick", [P, CB, 8])
        group_left = sb("group_left", [P, CB, GROUPS + 6])
        group_mask = sb("group_mask", [P, CB, GROUPS])
        masked = sb("masked", [P, CB, NE])
        expert_top = sb("expert_top", [P, CB, 8])
        expert_left = sb("expert_left", [P, CB, NE])
        weight = sb("weight", [P, 2, CB, NE])
        weight_sum = sb("weight_sum", [P, 2, CB])
        weight_inv = sb("weight_inv", [P, CB])
        rest = sb("rest", [P, 2, CB, NE])
        w_parts = sb("w_parts", [P, CB, 3, NE], BF16)
        w_parts_t = sb("w_parts_t", [3 * NE, 2, CT], BF16)

        bank = [stack.enter_context(nc.psum_tensor(f"bank{i}", [P, 512], F32)) for i in range(8)]
        scores_ps, st_ps, u_ps, ut_ps, small_ps = bank[0:2], bank[2:4], bank[4:6], bank[6], bank[7]
        gate_ps, up_ps, wbc_ps, y_ps, misc_ps = bank[0:2], bank[2:4], bank[4:6], bank[6], bank[7]

        x_in = [sem("x_in0"), sem("x_in1")]
        weights_in, small_in = sem("weights_in"), sem("small_in")
        keys_in = [sem(f"keys_in{b}") for b in range(CB)]
        raw_in = [sem(f"raw_in{b}") for b in range(CB)]
        wraw_in = [sem("wraw_in0"), sem("wraw_in1")]
        maxrow_in = [sem("maxrow_in0"), sem("maxrow_in1")]
        result_free = sem("result_free")
        zeroed, const_step, const_ready = sem("zeroed"), sem("const_step"), sem("const_ready")
        tanh_ready, bo_ready = sem("tanh_ready"), sem("bo_ready")
        fold_done, a_ready, ahi_ready, alo_ready, c_ready = (
            sem("fold_done"), sem("a_ready"), sem("ahi_ready"), sem("alo_ready"), sem("c_ready"))
        ln_step, xn_ready = sem("ln_step"), sem("xn_ready")
        xt_done, xhi_ready, xlo_ready = sem("xt_done"), sem("xhi_ready"), sem("xlo_ready")
        g_done, ghi_ready, glo_ready = sem("g_done"), sem("ghi_ready"), sem("glo_ready")
        diaghi_ready, diag_ready = sem("diaghi_ready"), sem("diag_ready")
        waits_passed, loads_begun = sem("waits_passed"), sem("loads_begun")
        wsplit_hi, wsplit_ready = sem("wsplit_hi"), sem("wsplit_ready")
        smax_done, max_ready = sem("smax_done"), sem("max_ready")
        maxt_done, maxt_ready = sem("maxt_done"), sem("maxt_ready")
        st_done, exp_ready = sem("st_done"), sem("exp_ready")
        u_done, inv_ready, norm_ready = sem("u_done"), sem("inv_ready"), sem("norm_ready")
        ut_done, ut_ready = sem("ut_done"), sem("ut_ready")
        attn_done, x2_ready = sem("attn_done"), sem("x2_ready")
        x2t_ready, x2hi_ready, x2lo_ready = sem("x2t_ready"), sem("x2hi_ready"), sem("x2lo_ready")
        logits_done, logits_ready, sig_ready = sem("logits_done"), sem("logits_ready"), sem("sig_ready")
        route_step, parts_ready = sem("route_step"), sem("parts_ready")
        wt_done, wt_ready = sem("wt_done"), sem("wt_ready")
        gate_done, up_done, wbc_done = sem("gate_done"), sem("up_done"), sem("wbc_done")
        silu_ready, gated_ready = sem("silu_ready"), sem("gated_ready")
        hid_ready, hidhi_ready, hidlo_ready = sem("hid_ready"), sem("hidhi_ready"), sem("hidlo_ready")
        down_done, yt_ready = sem("down_done"), sem("yt_ready")
        y_done, result_ready = sem("y_done"), sem("result_ready")

        def wait(eng, s, value):
            if isinstance(value, int) and value <= 0:
                return
            eng.wait_ge(s, value)

        x_dram = x.rearrange("b n d -> n b d")
        out_dram = out.rearrange("b n d -> n b d")

        def group(k):
            return slice(4 * (k // 2), 4 * (k // 2) + 4), k % 2

        def in_chunks(eng, body):
            body(0, True, False)
            with eng.Fori(1, NCH - 1) as c:
                body(c, False, False)
            body(NCH - 1, False, True)

        def in_chunk_pairs(eng, body):
            body(0, 0, True, False)
            with eng.Fori(0, NCH // 2 - 1) as i:
                body(2 * i + 1, 1, False, False)
                body(2 * i + 2, 0, False, False)
            body(NCH - 1, (NCH - 1) % 2, False, True)

        def free_of_2(c, u):
            return UNITS * c + (u - 1 if u >= 1 else 0)

        def free_of_slots(c, u):
            if u >= SLOTS:
                return UNITS * c + u - SLOTS + 1
            before = max(v for v in range(UNITS) if v % SLOTS == u)
            return UNITS * c - UNITS + before + 1

        block = stack.enter_context(nc.Block())

        @block.sync
        def _(sp):
            def wait_first(s, value):
                wait(sp, s, value)
                sp.sem_inc(loads_begun, 1)

            def load_keys(b, t):
                sp.dma_start(ctx_keys[:, b, 0:CD], ctx_nat[:, bass.ds(t, 1), :].rearrange("m a d -> m (a d)"))\
                    .then_inc(keys_in[b], 16)

            def load_raw(b, tokens):
                for q in range(2):
                    sp.dma_start(ctx_raw[q * CD:q * CD + CD, b, :], ctx_t[:, bass.ds(tokens, P)])\
                        .then_inc(raw_in[b], 16)

            def load_weights(slot, cols):
                sp.dma_start(w_raw[:, slot, :], experts[:, bass.ds(cols, WSTEP)]).then_inc(wraw_in[slot], 16)

            def load_max_row(t, parity, before):
                wait_first(maxt_ready, t + 1)
                wait_first(st_done, 4 * before + 4)
                sp.dma_start(raw(max_row[0:1, parity, :, :]), raw(max_t[:, parity, :])).then_inc(maxrow_in[parity], 16)

            sp.dma_start(x_sb[:, 0:CB, :], x_dram[:, 0:CB, :]).then_inc(x_in[0], 16)
            for n, g in enumerate((g_xattn, g_ffn)):
                sp.dma_start(gates[:, n:n + 1], g.rearrange("(a n) -> a n", a=1).broadcast_to([P, 1]))\
                    .then_inc(small_in, 16)
            sp.dma_start(bo_row[:], bo.rearrange("(a n) -> a n", a=1)).then_inc(small_in, 16)
            sp.dma_start(bias_bc[:], router_bias.rearrange("(a n) -> a n", a=1).broadcast_to([P, NE]))\
                .then_inc(small_in, 16)
            sp.dma_start(router_w[:], router_t).then_inc(small_in, 16)
            sp.dma_start(wq_pair, wq_t.rearrange("(p r) n -> r p n", r=P)).then_inc(weights_in, 16)
            sp.dma_start(wo_pair, wo.rearrange("(p r) n -> r p n", r=P)).then_inc(weights_in, 16)
            sp.wait_ge(zeroed, 2)
            for q in range(2):
                rows = slice(q * HD, q * HD + HD)
                for diag, w in ((wk_diag, wk_t), (wv_diag, wv_t)):
                    sp.dma_start(diag[rows, :, q * CD:q * CD + CD],
                                 w.rearrange("(p q r) n -> q r p n", q=2, r=HD)[q]).then_inc(weights_in, 16)
            for b in range(CB):
                load_raw(b, b * P)
            for b in range(CB - 1):
                load_keys(b, b)
            sp.dma_start(x_sb[:, CB:NB, :], x_dram[:, CB:NB, :]).then_inc(x_in[1], 16)
            for slot in range(2):
                load_weights(slot, slot * WSTEP)
            load_max_row(0, 0, -2)

            def attention(c, first, last):
                for b in range(CB):
                    t = CB * c + b
                    if not last:
                        wait_first(diag_ready, 2 * t + 2)
                        load_raw(b, (t + CB) * P)
                    if not (last and b >= 2):
                        wait_first(wsplit_ready, t + 1)
                        load_weights(b % 2, (t + 2) * WSTEP)
                    if not (last and b == CB - 1):
                        load_max_row(t + 1, (b + 1) % 2, t - 1)
                    if not (last and b > 0):
                        wait_first(u_done, 4 * t)
                        load_keys((b - 1) % CB, t - 1 + CB)

            in_chunks(sp, attention)

            sp.sem_inc(result_free, 16)
            with sp.Fori(0, NCH) as c:
                wait_first(result_ready, c + 1)
                sp.dma_start(out_dram[:, bass.ds(c * CB, CB), :], result.rearrange("p (b d) -> p b d", b=CB))\
                    .then_inc(result_free, 16)
            sp.wait_ge(result_free, 16 * NCH + 16)

        @block.gpsimd
        def _(pool):
            nc.gpsimd.memset(wk_diag, 0.0).then_inc(zeroed, 1)
            nc.gpsimd.memset(wv_diag, 0.0).then_inc(zeroed, 1)
            nc.gpsimd.memset(ones_col[:], 1.0).then_inc(const_step, 1)
            nc.gpsimd.memset(ident[:], 0.0).then_inc(const_step, 1)
            nc.gpsimd.memset(ident_bf[:], 0.0).then_inc(const_step, 1)
            nc.gpsimd.memset(expand[:], 0.0).then_inc(const_step, 1)
            nc.gpsimd.memset(raw(neg_ones[:]), -1.0).then_inc(const_ready, 1)
            nc.gpsimd.memset(ones_row[:], 1.0).then_inc(const_ready, 1)
            nc.gpsimd.memset(ctx_keys[:, :, CD:CD + 1], 1.0).then_inc(const_ready, 1)
            nc.gpsimd.memset(group_score[:], LOWEST).then_inc(const_ready, 1)
            nc.gpsimd.memset(group_pick[:], LOWEST).then_inc(const_ready, 1)
            pool.wait_ge(const_step, 4)
            for m in (ident, ident_bf):
                nc.gpsimd.affine_select(out=m[:], in_=m[:], compare_op=ALU.not_equal, fill=1.0, base=0,
                                        pattern=[[-1, P]], channel_multiplier=1).then_inc(const_ready, 1)
            nc.gpsimd.memset(raw(diag_hi[:]), 0.0).then_inc(zeroed, 1)
            nc.gpsimd.memset(raw(diag_lo[:]), 0.0).then_inc(zeroed, 1)

            def split_context(b, t, c):
                pool.wait_ge(raw_in[b], 32 * c + 32)
                wait(pool, wsplit_ready, t - CB + 1)
                wait(pool, st_done, 4 * (t - CB) + 4)
                for q in range(2):
                    rows = slice(q * CD, q * CD + CD)
                    nc.gpsimd.tensor_tensor(diag_hi[rows, b, q, :], ctx_raw[rows, b, :],
                                            ones_col[rows, :].broadcast_to([CD, P]), ALU.mult)\
                        .then_inc(diaghi_ready, 1)
                pool.wait_ge(diaghi_ready, 2 * t + 2)
                for q in range(2):
                    rows = slice(q * CD, q * CD + CD)
                    nc.gpsimd.tensor_tensor(diag_lo[rows, b, q, :], ctx_raw[rows, b, :],
                                            raw(diag_hi[rows, b, q, :]), ALU.subtract).then_inc(diag_ready, 1)

            def split_weights(slot, t, nth, contexts):
                cols = bass.ds(t * WSTEP, WSTEP)
                pool.wait_ge(wraw_in[slot], 16 * nth + 16)
                pool.wait_ge(diag_ready, contexts)
                nc.gpsimd.tensor_tensor(w_hi[:, cols], w_raw[:, slot, :], ones_col[:].broadcast_to([P, WSTEP]),
                                        ALU.mult).then_inc(wsplit_hi, 1)
                pool.wait_ge(wsplit_hi, t + 1)
                nc.gpsimd.tensor_tensor(w_lo[:, cols], w_raw[:, slot, :], raw(w_hi[:, cols]), ALU.subtract)\
                    .then_inc(wsplit_ready, 1)

            pool.wait_ge(zeroed, 4)
            for b in range(CB):
                split_context(b, b, 0)
            pool.wait_ge(diag_ready, 2 * CB)
            for part in range(3):
                rows = expand[part * NE:(part + 1) * NE].rearrange("j u (e i) -> j u e i", e=2)
                nc.gpsimd.affine_select(out=rows, in_=rows, compare_op=ALU.not_equal, fill=1.0, base=0,
                                        pattern=[[-2, NE // 2], [-1, 2], [0, EI]], channel_multiplier=1)\
                    .then_inc(const_ready, 1)
            pool.wait_ge(const_ready, 10)

            def attention(c, first, last):
                for b in range(CB):
                    t = CB * c + b
                    split_weights(b % 2, t, 2 * c + b // 2, 2 * NB if last else 2 * (t + CB))
                    if not last:
                        split_context(b, t + CB, c + 1)

            in_chunks(pool, attention)

            def experts_low(c):
                for u in range(UNITS):
                    n = UNITS * c + u
                    pool.wait_ge(hidhi_ready, n + 1)
                    wait(pool, down_done, free_of_slots(c, u))
                    nc.gpsimd.tensor_tensor(hid_lo[:, u % SLOTS, :], hid[:, u % 2, :], raw(hid_hi[:, u % SLOTS, :]),
                                            ALU.subtract).then_inc(hidlo_ready, 1)

            experts_low(0)
            with pool.Fori(1, NCH) as c:
                experts_low(c)

        @block.scalar
        def _(act):
            def xt_high(i):
                act.wait_ge(xt_done, i + 1)
                wait(act, g_done, 8 * i)
                nc.scalar.activation(xnt_hi[:], ut_ps[:], ACT.Copy).then_inc(xhi_ready, 1)

            def g_high(g, ring):
                for j in range(4):
                    act.wait_ge(g_done, 4 * g + j + 1)
                    wait(act, st_done, 8 * g - 8)
                    nc.scalar.activation(g_hi[:, ring, 2 * j:2 * j + 2, :],
                                         bank[j][:].rearrange("p (h n) -> p h n", h=2), ACT.Copy)\
                        .then_inc(ghi_ready, 1)

            def max_out(t, parity, loads_before):
                act.wait_ge(maxt_done, t + 1)
                wait(act, maxrow_in[parity], 16 * loads_before)
                nc.scalar.activation(max_t[:, parity, :], small_ps[0:HEADS, 0:P], ACT.Copy).then_inc(maxt_ready, 1)

            def ut_out(t, parity, r):
                act.wait_ge(ut_done, 2 * t + r + 1)
                wait(act, attn_done, t - 1)
                nc.scalar.activation(u_t[:, parity, 4 * r:4 * r + 4, :],
                                     ut_ps[:].rearrange("p (h n) -> p h n", h=4), ACT.Copy).then_inc(ut_ready, 1)

            act.wait_ge(small_in, 16 * 5)
            nc.scalar.activation(tanh_g[:], gates[:], ACT.Tanh).then_inc(tanh_ready, 1)
            act.wait_ge(tanh_ready, 1)
            nc.scalar.activation(bo_gated[:], bo_row[:], ACT.Copy, scale=tanh_g[0:1, 0:1]).then_inc(bo_ready, 1)
            for i in range(2):
                act.wait_ge(fold_done, i + 1)
                half = slice(4 * i, 4 * i + 4)
                nc.scalar.activation(a_full[:, half, :], bank[i][:].rearrange("p (h n) -> p h n", h=4), ACT.Copy,
                                     scale=SCALE).then_inc(a_ready, 1)
                act.wait_ge(a_ready, i + 1)
                nc.scalar.activation(a_hi[:, half, :], a_full[:, half, :], ACT.Copy).then_inc(ahi_ready, 1)
            xt_high(0)
            for i in range(2):
                act.wait_ge(fold_done, i + 3)
                nc.scalar.activation(c_pair[:, 4 * i:4 * i + 4, :], bank[2 + i][:].rearrange("p (h n) -> p h n", h=4),
                                     ACT.Copy, scale=tanh_g[:, 0:1]).then_inc(c_ready, 1)
            for ring in range(2):
                g_high(ring, ring)
            max_out(0, 0, 0)

            def attention(c, first, last):
                for b in range(CB):
                    t = CB * c + b
                    for k in range(4):
                        if k == 1 and not (last and b == CB - 1):
                            max_out(t + 1, (b + 1) % 2, 2 * c + (b - 1) // 2 + 1)
                        act.wait_ge(st_done, 4 * t + k + 1)
                        wait(act, u_done, 4 * t + k - 3)
                        nc.scalar.activation(probs_t[:, k, :, :],
                                             st_ps[k % 2][:].rearrange("p (h n) -> p h n", h=4), ACT.Exp)\
                            .then_inc(exp_ready, 1)
                        if b == 1 and k == 0 and not last:
                            xt_high(c + 1)
                        if k == 2 and not (first and b == 0):
                            ut_out(t - 1, (b - 1) % 2, 1)
                        if k == 3:
                            ut_out(t, b % 2, 0)
                    if b % 2 == 1 and not last:
                        g_high(2 * c + 2 + b // 2, b // 2)

            in_chunks(act, attention)
            ut_out(NB - 1, (NB - 1) % 2, 1)

            def x2t_out(c):
                act.wait_ge(xt_done, NCH + c + 1)
                nc.scalar.activation(x2t, misc_ps[:], ACT.Copy).then_inc(x2t_ready, 1)

            def x2t_high(c, parity):
                act.wait_ge(x2t_ready, c + 1)
                wait(act, up_done, UNITS * (c - 1))
                nc.scalar.activation(x2t_hi[:, parity, :], x2t, ACT.Copy).then_inc(x2hi_ready, 1)

            def logits_out(c):
                act.wait_ge(logits_done, c + 1)
                nc.scalar.activation(logits[:], misc_ps[:, 0:CB * NE], ACT.Copy).then_inc(logits_ready, 1)

            def sigmoids(c):
                act.wait_ge(logits_ready, c + 1)
                nc.scalar.activation(tanh_half[:], logits[:], ACT.Tanh, scale=0.5).then_inc(sig_ready, 1)
                act.wait_ge(route_step, ROUTE_STEPS * c + 1)
                nc.scalar.activation(silu_low[:], logits_low[:], ACT.Silu).then_inc(sig_ready, 1)

            def weights_out(c, parity):
                act.wait_ge(wt_done, c + 1)
                wait(act, wbc_done, (UNITS - 1) * (c - 1))
                nc.scalar.activation(w_parts_t[:, parity, :], misc_ps[:].bitcast(BF16)[0:3 * NE, 0:CT], ACT.Copy)\
                    .then_inc(wt_ready, 1)

            def hidden_high(c, u):
                act.wait_ge(hid_ready, UNITS * c + u + 1)
                wait(act, down_done, free_of_slots(c, u))
                nc.scalar.activation(hid_hi[:, u % SLOTS, :], hid[:, u % 2, :], ACT.Copy).then_inc(hidhi_ready, 1)

            def y_out(c):
                act.wait_ge(down_done, UNITS * (c + 1))
                nc.scalar.activation(y_t, y_ps[:], ACT.Copy).then_inc(yt_ready, 1)

            def experts_of(c, parity, first, last):
                for u in range(UNITS):
                    act.wait_ge(gate_done, UNITS * c + u + 1)
                    wait(act, gated_ready, free_of_2(c, u))
                    nc.scalar.activation(silu_g[:, u % 2, :], gate_ps[u % 2][:], ACT.Silu).then_inc(silu_ready, 1)
                    if u >= 1:
                        hidden_high(c, u - 1)
                    if u == 0:
                        weights_out(c, parity)
                    if u == LAG and not first:
                        y_out(c - 1)
                    if not last:
                        if u == 4:
                            x2t_out(c + 1)
                        if u == 5:
                            x2t_high(c + 1, 1 - parity)
                        if u == 6:
                            logits_out(c + 1)
                        if u == 8:
                            sigmoids(c + 1)
                hidden_high(c, UNITS - 1)

            x2t_out(0)
            x2t_high(0, 0)
            logits_out(0)
            sigmoids(0)
            in_chunk_pairs(act, experts_of)
            y_out(NCH - 1)

        @block.vector
        def _(dve):
            def wait_first(s, value):
                dve.wait_ge(s, value)
                dve.sem_inc(waits_passed, 1)

            def ln_stats(n, t):
                for i in range(CB):
                    nc.vector.bn_stats(bn6[:, i, :], x_sb[:, bass.ds(t + i, 1), :].rearrange("p a d -> p (a d)"))\
                        .then_inc(ln_step, 1)
                for i in range(CB):
                    wait_first(ln_step, LN_STEPS * n + i + 1)
                    nc.vector.bn_aggr(mean_var[:, i, :], bn6[:, i, :]).then_inc(ln_step, 1)
                dve.wait_ge(ln_step, LN_STEPS * n + 2 * CB)
                nc.vector.tensor_scalar(var_eps[:], mean_var[:, :, 1], EPS, None, ALU.add).then_inc(ln_step, 1)

            def ln_guess(n):
                dve.wait_ge(ln_step, LN_STEPS * n + 2 * CB + 1)
                nc.vector.tensor_scalar(rsqrt_bits[:].bitcast(I32), var_eps[:].bitcast(I32), 1, 0x7fffffff,
                                        ALU.logical_shift_right, ALU.bitwise_xor).then_inc(ln_step, 1)
                nc.vector.tensor_scalar(half_var[:], var_eps[:], -0.5, None, ALU.mult).then_inc(ln_step, 1)
                dve.wait_ge(ln_step, LN_STEPS * n + 2 * CB + 3)
                nc.vector.tensor_scalar(guess[:, 0, :], rsqrt_bits[:], GUESS_SCALE, None, ALU.mult).then_inc(ln_step, 1)

            def ln_newton(n, i):
                at = LN_STEPS * n + 2 * CB + 4 + 3 * i
                r, better = guess[:, i, :], rstd[:] if i == NEWTON_STEPS - 1 else guess[:, i + 1, :]
                dve.wait_ge(ln_step, at)
                nc.vector.tensor_tensor(newton[:, 0, :], r, r, ALU.mult).then_inc(ln_step, 1)
                dve.wait_ge(ln_step, at + 1)
                nc.vector.tensor_tensor(newton[:, 1, :], newton[:, 0, :], half_var[:], ALU.mult).then_inc(ln_step, 1)
                dve.wait_ge(ln_step, at + 2)
                nc.vector.scalar_tensor_tensor(better, newton[:, 1, :], 1.5, r, ALU.add, ALU.mult).then_inc(ln_step, 1)

            def layer_norm(n, t):
                ln_stats(n, t)
                ln_guess(n)
                for i in range(NEWTON_STEPS):
                    ln_newton(n, i)
                ln_apply(n, t)

            def ln_apply(n, t):
                dve.wait_ge(ln_step, LN_STEPS * n + LN_STEPS)
                wait(dve, xt_done, n)
                for i in range(CB):
                    nc.vector.tensor_scalar(xn[:, i, :], x_sb[:, bass.ds(t + i, 1), :].rearrange("p a d -> p (a d)"),
                                            mean_var[:, i, 0:1], rstd[:, i:i + 1], ALU.subtract, ALU.mult)\
                        .then_inc(xn_ready, 1)

            def xt_low(i):
                dve.wait_ge(xhi_ready, i + 1)
                nc.vector.tensor_tensor(xnt_lo[:], ut_ps[:], raw(xnt_hi[:]), ALU.subtract).then_inc(xlo_ready, 1)

            def g_low(g, ring):
                for j in range(4):
                    dve.wait_ge(ghi_ready, 4 * g + j + 1)
                    nc.vector.tensor_tensor(g_lo[:, ring, 2 * j:2 * j + 2, :],
                                            bank[j][:].rearrange("p (h n) -> p h n", h=2),
                                            raw(g_hi[:, ring, 2 * j:2 * j + 2, :]), ALU.subtract)\
                        .then_inc(glo_ready, 1)

            def take_max(t, parity, k):
                dve.wait_ge(smax_done, 4 * t + k + 1)
                wait(dve, maxt_done, t - 1)
                nc.vector.tensor_reduce(row_max[:, parity, 4 * k:4 * k + 4],
                                        scores_ps[k % 2][:].rearrange("p (h m) -> p h m", h=4), AX_X, ALU.max)\
                    .then_inc(max_ready, 1)

            def normalise(t, parity, k):
                pairs, q = group(k)
                u = u_ps[k % 2][:, 0:4 * (CD + 1)].rearrange("p (h d) -> p h d", h=4)
                dve.wait_ge(u_done, 4 * t + k + 1)
                wait(dve, inv_ready, 4 * t + k - 3)
                nc.vector.reciprocal(inv_sum[:, k, :], u[:, :, CD]).then_inc(inv_ready, 1)
                dve.wait_ge(inv_ready, 4 * t + k + 1)
                wait(dve, ut_done, 2 * (t - 2) + k // 2 + 1)
                nc.vector.tensor_tensor(u_norm[:, parity, pairs, q, :], u[:, :, 0:CD],
                                        inv_sum[:, k, :].unsqueeze(2).broadcast_to([P, 4, CD]), ALU.mult)\
                    .then_inc(norm_ready, 1)

            def residual(t):
                dve.wait_ge(attn_done, t + 1)
                tile = x_sb[:, bass.ds(t, 1), :].rearrange("p a d -> p (a d)")
                nc.vector.tensor_tensor(tile, small_ps[:, D:2 * D], tile, ALU.add).then_inc(x2_ready, 1)

            dve.wait_ge(x_in[0], 16)
            layer_norm(0, 0)
            for i in range(2):
                dve.wait_ge(ahi_ready, i + 1)
                half = slice(4 * i, 4 * i + 4)
                nc.vector.tensor_tensor(a_lo[:, half, :], a_full[:, half, :], raw(a_hi[:, half, :]), ALU.subtract)\
                    .then_inc(alo_ready, 1)
            xt_low(0)
            for ring in range(2):
                g_low(ring, ring)
            dve.wait_ge(x_in[1], 16)
            for b in range(2):
                for k in range(4):
                    take_max(b, b, k)

            def attention(c, first, last):
                for b in range(CB):
                    t = CB * c + b
                    for k in range(4):
                        if not (last and b >= 2):
                            take_max(t + 2, b % 2, k)
                        if k > 0:
                            normalise(t, b % 2, k - 1)
                        elif not (first and b == 0):
                            normalise(t - 1, (b - 1) % 2, 3)
                        if k == 0 and not (first and b < 2):
                            residual(t - 2)
                        if b == 0 and not last:
                            if k == 0:
                                ln_stats(c + 1, t + CB)
                            if k == 1:
                                ln_guess(c + 1)
                            if k >= 1:
                                ln_newton(c + 1, k - 1)
                            if k == 3:
                                ln_apply(c + 1, t + CB)
                        if b == 1 and k == 1 and not last:
                            xt_low(c + 1)
                    if b % 2 == 1 and not last:
                        g_low(2 * c + 2 + b // 2, b // 2)

            in_chunks(dve, attention)
            normalise(NB - 1, (NB - 1) % 2, 3)
            residual(NB - 2)
            residual(NB - 1)

            def step(ins):
                ins.then_inc(route_step, 1)
                counted[0] += 1

            def so_far(c, alone=False):
                (wait_first if alone else dve.wait_ge)(route_step, ROUTE_STEPS * c + counted[0])

            counted = [0]

            def route_low(c):
                counted[0] = 0
                dve.wait_ge(logits_ready, c + 1)
                step(nc.vector.tensor_scalar(logits_low[:], logits[:], -1.0, None, ALU.min))

            def route_scores(c):
                low_inv, high, low, rise, risen = (sig[:, i, :] for i in range(5))
                dve.wait_ge(sig_ready, 2 * c + 2)
                step(nc.vector.reciprocal(low_inv, logits_low[:]))
                step(nc.vector.tensor_scalar(high, tanh_half[:], 0.5, 0.5, ALU.mult, ALU.add))
                so_far(c)
                step(nc.vector.tensor_tensor(low, silu_low[:], low_inv, ALU.mult))
                so_far(c)
                step(nc.vector.tensor_tensor(rise, high, low, ALU.subtract))
                so_far(c)
                step(nc.vector.scalar_tensor_tensor(risen, logits[:], -1.0, rise, ALU.is_gt, ALU.mult))
                so_far(c)
                step(nc.vector.tensor_tensor(flat(score[:], 3), low, risen, ALU.add))
                so_far(c)
                step(nc.vector.tensor_tensor(choice[:], score[:], bias_bc[:].unsqueeze(1).broadcast_to([P, CB, NE]),
                                             ALU.add))

            def route_groups(c):
                so_far(c, alone=True)
                for i in range(CB):
                    for g in range(GROUPS):
                        step(nc.vector.max(top_in_group[:, i, g, :], choice[:, i, g * GE:(g + 1) * GE]))
                so_far(c)
                step(nc.vector.tensor_tensor(group_score[:, :, 0:GROUPS], top_in_group[:, :, :, 0],
                                             top_in_group[:, :, :, 1], ALU.add))

            def route_pick_groups(c):
                so_far(c, alone=True)
                for i in range(CB):
                    step(nc.vector.max(group_top[:, i, :], group_score[:, i, :]))
                so_far(c)
                step(nc.vector.tensor_copy(group_pick[:, :, 0:GROUPS_TAKEN], group_top[:, :, 0:GROUPS_TAKEN]))
                so_far(c, alone=True)
                for i in range(CB):
                    step(nc.vector.match_replace(group_left[:, i, :], group_pick[:, i, :], group_score[:, i, :], PICKED))

            def route_mask(c):
                so_far(c)
                step(nc.vector.tensor_scalar(group_mask[:], group_left[:, :, 0:GROUPS], PICKED, None, ALU.is_equal))
                so_far(c)
                step(nc.vector.tensor_tensor(
                    flat(masked[:], 3).rearrange("p (b e) -> p b e", e=GE),
                    flat(choice[:], 3).rearrange("p (b e) -> p b e", e=GE),
                    flat(group_mask[:], 3).unsqueeze(2).broadcast_to([P, CB * GROUPS, GE]), ALU.mult))

            def route_pick_experts(c):
                so_far(c, alone=True)
                for i in range(CB):
                    step(nc.vector.max(expert_top[:, i, :], masked[:, i, :]))
                so_far(c, alone=True)
                for i in range(CB):
                    step(nc.vector.match_replace(expert_left[:, i, :], expert_top[:, i, :], masked[:, i, :], PICKED))

            def route_weights(c):
                so_far(c)
                step(nc.vector.scalar_tensor_tensor(flat(weight[:, 0], 3), flat(expert_left[:], 3), PICKED,
                                                    flat(score[:], 3), ALU.is_equal, ALU.mult))
                so_far(c)
                step(nc.vector.tensor_reduce(weight_sum[:, 0, :], weight[:, 0], AX_X, ALU.add))
                so_far(c)
                step(nc.vector.tensor_scalar(weight_sum[:, 1, :], weight_sum[:, 0, :], 1e-20, None, ALU.add))
                so_far(c)
                step(nc.vector.reciprocal(weight_inv[:], weight_sum[:, 1, :]))
                so_far(c)
                step(nc.vector.scalar_tensor_tensor(weight[:, 1], weight[:, 0], ROUTED_SCALING,
                                                    weight_inv[:].unsqueeze(2).broadcast_to([P, CB, NE]),
                                                    ALU.mult, ALU.mult))

            def route_parts(c):
                so_far(c)
                wait(dve, wt_done, c)
                step(nc.vector.tensor_copy(w_parts[:, :, 0, :], weight[:, 1]))
                so_far(c)
                step(nc.vector.tensor_tensor(rest[:, 0], weight[:, 1], w_parts[:, :, 0, :], ALU.subtract))
                so_far(c)
                step(nc.vector.tensor_copy(w_parts[:, :, 1, :], rest[:, 0]))
                so_far(c)
                step(nc.vector.tensor_tensor(rest[:, 1], rest[:, 0], w_parts[:, :, 1, :], ALU.subtract))
                so_far(c)
                nc.vector.tensor_copy(w_parts[:, :, 2, :], rest[:, 1]).then_inc(parts_ready, 1)
                assert counted[0] == ROUTE_STEPS

            def x2t_low(c, parity):
                dve.wait_ge(x2hi_ready, c + 1)
                nc.vector.tensor_tensor(x2t_lo[:, parity, :], x2t, raw(x2t_hi[:, parity, :]), ALU.subtract)\
                    .then_inc(x2lo_ready, 1)

            route_stages = (route_scores, route_groups, route_pick_groups, route_mask, route_pick_experts,
                            route_weights, route_parts)

            def result_of(c):
                dve.wait_ge(y_done, c + 1)
                dve.wait_ge(result_free, 16 * c + 16)
                nc.vector.scalar_tensor_tensor(
                    result, misc_ps[:], tanh_g[:, 1:2],
                    x_sb[:, bass.ds(CB * c, CB), :].rearrange("p b d -> p (b d)"), ALU.mult, ALU.add)\
                    .then_inc(result_ready, 1)

            def experts_of(c, parity, first, last):
                for u in range(UNITS):
                    n = UNITS * c + u
                    dve.wait_ge(silu_ready, n + 1)
                    dve.wait_ge(up_done, n + 1)
                    wait(dve, hid_ready, free_of_2(c, u))
                    nc.vector.tensor_tensor(gated[:, u % 2, :], silu_g[:, u % 2, :], up_ps[u % 2][:], ALU.mult)\
                        .then_inc(gated_ready, 1)
                    dve.wait_ge(gated_ready, n + 1)
                    wait(dve, hidlo_ready, free_of_2(c, u))
                    if u == 0:
                        nc.vector.tensor_copy(hid[:, u % 2, :], gated[:, u % 2, :]).then_inc(hid_ready, 1)
                    else:
                        dve.wait_ge(wbc_done, (UNITS - 1) * c + u)
                        nc.vector.tensor_tensor(hid[:, u % 2, :], gated[:, u % 2, :], wbc_ps[u % 2][:], ALU.mult)\
                            .then_inc(hid_ready, 1)
                    if u == 8 and not first:
                        result_of(c - 1)
                    if not last:
                        if u == 0:
                            ln_stats(NCH + c + 1, CB * (c + 1))
                        if u == 1:
                            ln_guess(NCH + c + 1)
                        if u in (1, 2, 3):
                            ln_newton(NCH + c + 1, u - 1)
                        if u == 3:
                            ln_apply(NCH + c + 1, CB * (c + 1))
                        if u == 6:
                            x2t_low(c + 1, 1 - parity)
                        if u == 7:
                            route_low(c + 1)
                        if 9 <= u < 9 + len(route_stages):
                            route_stages[u - 9](c + 1)

            layer_norm(NCH, 0)
            dve.wait_ge(const_ready, 10)
            dve.wait_ge(small_in, 16 * 5)
            x2t_low(0, 0)
            route_low(0)
            for stage in route_stages:
                stage(0)
            in_chunk_pairs(dve, experts_of)
            result_of(NCH - 1)

        @block.tensor
        def _(pe):
            def split_product(ps, w, x, start=True, stop=True):
                (wh, wl), (xh, xl) = w, x
                nc.tensor.matmul(ps, wh, xh, start=start, stop=False)
                nc.tensor.matmul(ps, wl, xh, start=False, stop=False)
                return nc.tensor.matmul(ps, wh, xl, start=False, stop=stop)

            def transpose_norm(n, ps):
                pe.wait_ge(xn_ready, CB * n + CB)
                for i in range(CB):
                    ins = nc.tensor.transpose(ps[:, i * P:(i + 1) * P], xn[:, i, :], ident[:])
                ins.then_inc(xt_done, 1)

            def g_project(ring, chunk, bank_free):
                pe.wait_ge(xlo_ready, chunk + 1)
                for j in range(4):
                    s, value = bank_free[j // 2]
                    wait(pe, s, value + j % 2)
                    for i in range(2):
                        p = 2 * j + i
                        cols = slice(ring * 2 * P, (ring + 1) * 2 * P)
                        ins = split_product(bank[j][:, i * 2 * P:(i + 1) * 2 * P],
                                            (a_hi[:, p, :], a_lo[:, p, :]), (xnt_hi[:, cols], xnt_lo[:, cols]))
                    ins.then_inc(g_done, 1)

            def max_scores(t, b, half, k):
                pe.wait_ge(ghi_ready, 4 * half + k + 1)
                if b % 2 == 0 and k < 2:
                    pe.wait_ge(glo_ready, 4 * half + k + 1)
                wait(pe, max_ready, 4 * t + k - 1)
                pe.wait_ge(diag_ready, 2 * t + 2)
                for i in range(2):
                    ins = nc.tensor.matmul(scores_ps[k % 2][:, i * 2 * P:(i + 1) * 2 * P],
                                           g_hi[:, (b // 2) % 2, 2 * k + i, (b % 2) * P:(b % 2 + 1) * P],
                                           flat(diag_hi[:, b % CB, :, :], 3), start=True, stop=True)
                ins.then_inc(smax_done, 1)

            def transpose_max(t, parity):
                pe.wait_ge(max_ready, 4 * t + 4)
                wait(pe, x2_ready, t - 2)
                wait(pe, maxt_ready, t)
                nc.tensor.transpose(small_ps[0:HEADS, 0:P], row_max[:, parity, :], ident[:]).then_inc(maxt_done, 1)

            def scores(t, b, half, k, loads, projections):
                pairs, q = group(k)
                ps = st_ps[k % 2][:]
                if k == 0:
                    pe.wait_ge(maxrow_in[b % 2], 16 * loads)
                    pe.wait_ge(glo_ready, 4 * half + 4)
                wait(pe, exp_ready, 4 * t + k - 1)
                if projections is not None and k < 2:
                    pe.wait_ge(glo_ready, 4 * projections + k - 1)
                cols = slice((b % 2) * P, (b % 2 + 1) * P)
                split_product(ps, (diag_hi[:, b, q, :], diag_lo[:, b, q, :]),
                              (g_hi[:, b // 2, pairs, cols], g_lo[:, b // 2, pairs, cols]), stop=False)
                heads = max_row[0:1, b % 2, :, :].rearrange("a (h q) n -> a h q n", q=2)
                nc.tensor.matmul(ps, neg_ones[:], heads[:, pairs, q, :], start=False, stop=True).then_inc(st_done, 1)

            def weigh(t, b, k, loads):
                pe.wait_ge(exp_ready, 4 * t + k + 1)
                wait(pe, norm_ready, 4 * t + k - 1)
                if k == 0:
                    pe.wait_ge(keys_in[b], 16 * loads)
                for i in range(4):
                    ins = nc.tensor.matmul(u_ps[k % 2][:, i * (CD + 1):(i + 1) * (CD + 1)], probs_t[:, k, i, :],
                                           ctx_keys[:, b, :], start=True, stop=True)
                ins.then_inc(u_done, 1)

            def transpose_u(t, parity, r):
                pe.wait_ge(norm_ready, 4 * t + 2 * r + 2)
                wait(pe, ut_ready, 2 * t + r)
                for i in range(4):
                    ins = nc.tensor.transpose(ut_ps[:, i * P:(i + 1) * P],
                                              u_norm[:, parity, 4 * r + i, :, :].rearrange("p q d -> p (q d)"), ident[:])
                ins.then_inc(ut_done, 1)

            def project_out(t, parity, maxima):
                pe.wait_ge(ut_ready, 2 * t + 2)
                pe.wait_ge(maxt_ready, maxima)
                ps = small_ps[:, D:2 * D]
                nc.tensor.matmul(ps, ones_row[:], bo_gated[:], start=True, stop=False)
                for p in range(PAIRS):
                    ins = nc.tensor.matmul(ps, u_t[:, parity, p, :], c_pair[:, p, :], start=False, stop=p == PAIRS - 1)
                ins.then_inc(attn_done, 1)

            pe.wait_ge(weights_in, 16 * 6)
            for i in range(4):
                left, right = ((wq_pair, wk_diag), (wv_diag, wo_pair))[i // 2]
                for j in range(4):
                    p = 4 * (i % 2) + j
                    ins = nc.tensor.matmul(bank[i][:, j * P:(j + 1) * P], left[:, p, :], right[:, p, :],
                                           start=True, stop=True)
                ins.then_inc(fold_done, 1)
            pe.wait_ge(const_ready, 7)
            transpose_norm(0, ut_ps)
            pe.wait_ge(alo_ready, 2)
            pe.wait_ge(c_ready, 2)
            pe.wait_ge(bo_ready, 1)
            g_project(0, 0, ((glo_ready, -2), (glo_ready, -2)))
            g_project(1, 0, ((glo_ready, 1), (glo_ready, 3)))
            for b in range(2):
                for k in range(4):
                    if b == 0 and k < 2:
                        pe.wait_ge(glo_ready, 8)
                    max_scores(b, b, 0, k)
            transpose_max(0, 0)

            def attention(c, first, last):
                for b in range(CB):
                    t = CB * c + b
                    for k in range(4):
                        if k == 1 and not (last and b == CB - 1):
                            transpose_max(t + 1, (b + 1) % 2)
                        if b == 1 and k == 0 and not last:
                            pe.wait_ge(ut_ready, 2 * (t - 1) + 1)
                            transpose_norm(c + 1, ut_ps)
                        if not (last and b >= 2):
                            max_scores(t + 2, b + 2, 2 * c + (b + 2) // 2, k)
                        if k == 0 and not (first and b == 0):
                            weigh(t - 1, (b - 1) % CB, 3, c + 1)
                        projections = {0: 2 * c + 2, 2: None if last else 2 * c + 3}.get(b)
                        scores(t, b, 2 * c + b // 2, k, 2 * c + b // 2 + 1, projections)
                        if k > 0:
                            weigh(t, b, k - 1, c + 1)
                        if k == 2 and not (first and b == 0):
                            if b == 1 and not last:
                                pe.wait_ge(xlo_ready, c + 2)
                            transpose_u(t - 1, (b - 1) % 2, 1)
                        if k == 3:
                            transpose_u(t, b % 2, 0)
                            if not (first and b == 0):
                                project_out(t - 1, (b - 1) % 2, t + 1 if last and b == CB - 1 else t + 2)
                    if b % 2 == 1 and not last:
                        g_project(b // 2, c + 1, ((max_ready, 4 * (t + 2) + 3), (exp_ready, 4 * t + 3)))

            in_chunks(pe, attention)
            weigh(NB - 1, CB - 1, 3, NCH)
            transpose_u(NB - 1, (NB - 1) % 2, 1)
            pe.wait_ge(x2_ready, NB - 1)
            project_out(NB - 1, (NB - 1) % 2, NB)

            def weight_halves(kind, u):
                cols = slice(kind * FW + u * P, kind * FW + (u + 1) * P)
                return w_hi[:, cols], w_lo[:, cols]

            x2_halves = [(x2t_hi[:, i, :], x2t_lo[:, i, :]) for i in range(2)]

            def route(c):
                pe.wait_ge(x2t_ready, c + 1)
                for i in range(CB):
                    ins = nc.tensor.matmul(misc_ps[:, i * NE:(i + 1) * NE], x2t[:, i * P:(i + 1) * P], router_w[:],
                                           start=True, stop=True)
                ins.then_inc(logits_done, 1)

            def transpose_weights(c):
                pe.wait_ge(parts_ready, c + 1)
                pe.wait_ge(logits_ready, c + 1)
                if not isinstance(c, int) or c > 1:
                    pe.wait_ge(result_ready, c - 1)
                ps = misc_ps[:].bitcast(BF16)
                for i in range(CB):
                    ins = nc.tensor.transpose(ps[0:3 * NE, i * P:(i + 1) * P],
                                              w_parts[:, i, :, :].rearrange("p a e -> p (a e)"), ident_bf[:])
                ins.then_inc(wt_done, 1)

            def down(c, u):
                n = UNITS * c + u
                pe.wait_ge(hidlo_ready, n + 1)
                if u == 0:
                    wait(pe, yt_ready, c)
                split_product(y_ps[:], weight_halves(2, u), (hid_hi[:, u % SLOTS, :], hid_lo[:, u % SLOTS, :]),
                              start=u == 0, stop=u == UNITS - 1).then_inc(down_done, 1)

            def transpose_y(c):
                pe.wait_ge(yt_ready, c + 1)
                for i in range(CB):
                    ins = nc.tensor.transpose(misc_ps[:, i * P:(i + 1) * P], y_t[:, i * P:(i + 1) * P], ident[:])
                ins.then_inc(y_done, 1)

            def experts_of(c, parity, first, last):
                for u in range(UNITS):
                    n = UNITS * c + u
                    if u == 0:
                        pe.wait_ge(x2lo_ready, c + 1)
                    wait(pe, silu_ready, free_of_2(c, u))
                    split_product(gate_ps[u % 2][:], weight_halves(0, u), x2_halves[parity]).then_inc(gate_done, 1)
                    wait(pe, gated_ready, free_of_2(c, u))
                    split_product(up_ps[u % 2][:], weight_halves(1, u), x2_halves[parity]).then_inc(up_done, 1)
                    if u > 0:
                        if u == 1:
                            pe.wait_ge(wt_ready, c + 1)
                        wait(pe, hid_ready, free_of_2(c, u))
                        nc.tensor.matmul(wbc_ps[u % 2][:], expand[:, u - 1, :], w_parts_t[:, parity, :],
                                         start=True, stop=True).then_inc(wbc_done, 1)
                    if u >= LAG:
                        down(c, u - LAG)
                    elif not first:
                        down(c - 1, UNITS - LAG + u)
                    if u == 0:
                        transpose_weights(c)
                    if u == 3 and not last:
                        pe.wait_ge(wt_ready, c + 1)
                        transpose_norm(NCH + c + 1, misc_ps)
                    if u == 5 and not last:
                        route(c + 1)
                    if u == 7 and not first:
                        if last:
                            pe.wait_ge(wt_ready, c + 1)
                        else:
                            pe.wait_ge(logits_ready, c + 2)
                        transpose_y(c - 1)

            pe.wait_ge(x2_ready, NB)
            pe.wait_ge(wsplit_ready, NB)
            pe.wait_ge(const_ready, 10)
            transpose_norm(NCH, misc_ps)
            route(0)
            in_chunk_pairs(pe, experts_of)
            for u in range(UNITS - LAG, UNITS):
                down(NCH - 1, u)
            transpose_y(NCH - 1)


def kernel(x, ctx_512, g_xattn, g_ffn, L0_xattn_Wq, L0_xattn_Wk, L0_xattn_Wv, L0_xattn_Wo, L0_xattn_bo,
           L0_ffn_gate_w, L0_ffn_gate_bias, L0_ffn_expert_gate, L0_ffn_expert_up, L0_ffn_expert_down,
           L0_ffn_shared_gate, L0_ffn_shared_up, L0_ffn_shared_down):
    import numpy as np
    import concourse.bacc as bacc
    from concourse.bass_utils import run_bass_kernel_spmd

    lay = np.ascontiguousarray
    ctx = np.asarray(ctx_512)

    def up(w, shared):
        return np.concatenate([np.asarray(shared).T, np.asarray(w).reshape(NE * EI, D).T], axis=1)

    down = np.concatenate([np.asarray(L0_ffn_shared_down).T,
                           np.asarray(L0_ffn_expert_down).transpose(0, 2, 1).reshape(NE * EI, D)], axis=0)
    down = down.reshape(UNITS, P, D).transpose(1, 0, 2).reshape(P, FW)
    experts = np.concatenate([up(L0_ffn_expert_gate, L0_ffn_shared_gate), up(L0_ffn_expert_up, L0_ffn_shared_up), down],
                             axis=1)
    arrays = {
        "x": lay(x), "ctx_nat": lay(ctx.transpose(1, 0, 2)), "ctx_t": lay(ctx.reshape(NB * P, CD).T),
        "g_xattn": lay(g_xattn), "g_ffn": lay(g_ffn), "wq_t": lay(np.asarray(L0_xattn_Wq).T),
        "wk_t": lay(np.asarray(L0_xattn_Wk).T), "wv_t": lay(np.asarray(L0_xattn_Wv).T), "wo": lay(L0_xattn_Wo),
        "bo": lay(L0_xattn_bo), "router_t": lay(np.asarray(L0_ffn_gate_w).T), "router_bias": lay(L0_ffn_gate_bias),
        "experts": lay(experts),
    }
    nc = bacc.Bacc("TRN2", target_bir_lowering=False, num_devices=1)
    ins = [nc.dram_tensor(n, a.shape, F32, kind="ExternalInput").ap() for n, a in arrays.items()]
    out = nc.dram_tensor("out", (NB, P, D), F32, kind="ExternalOutput").ap()
    build(nc, *ins, out)
    r = run_bass_kernel_spmd(nc, [arrays], core_ids=[0])
    return r.results[0]["out"]
```

```python
from contextlib import ExitStack

import concourse.bass as bass
from concourse import mybir

F32 = mybir.dt.float32
F32R = mybir.dt.float32r
BF16 = mybir.dt.bfloat16
I32 = mybir.dt.int32
ACT = mybir.ActivationFunctionType
ALU = mybir.AluOpType
AX_X = mybir.AxisListType.X

P = 128
NB = 32
D = 128
HEADS, HD, CD = 16, 64, 64
PAIRS = HEADS // 2
CB = 4
NCH = NB // CB
CT = CB * P
NE, EI = 32, 64
GROUPS, GE = 4, 8
GROUPS_TAKEN = 2
UNITS = NE // 2 + 1
FW = UNITS * P
WCOLS = 3 * FW
WSTEP = WCOLS // NB
SCALE = float(HD) ** -0.5
ROUTED_SCALING = 2.5
EPS = 1e-5
LOWEST, PICKED = -1.0e30, 3.0e38
GUESS_SCALE = 1.36 * 2.0 ** -66

NEWTON_STEPS = 3
LN_STEPS = 2 * CB + 4 + 3 * NEWTON_STEPS
ROUTE_STEPS = 53
LAG = 4
SLOTS = 4
HIDS = 3
LN_LEVELS = 6 + 3 * NEWTON_STEPS
LN_SPREAD = 5


def build(nc, x, ctx_nat, ctx_t, g_xattn, g_ffn, wq_t, wk_t, wv_t, wo, bo, router_t, router_bias, experts, out):
    with ExitStack() as stack:
        def sb(name, shape, dt=F32):
            return stack.enter_context(nc.sbuf_tensor(name, shape, dt))

        def sem(name):
            return stack.enter_context(nc.semaphore(name))

        def raw(ap):
            return ap.bitcast(F32)

        def flat(ap, n):
            return ap.rearrange({3: "p a b -> p (a b)", 4: "p a b c -> p (a b c)"}[n])

        x_sb = sb("x_sb", [P, NB, D])
        ident = sb("ident", [P, P])
        ident_bf = sb("ident_bf", [P, P], BF16)
        neg_ones = sb("neg_ones", [1, P], F32R)
        ones_row = sb("ones_row", [1, P])
        ones_col = sb("ones_col", [P, 1])
        gates = sb("gates", [P, 2])
        tanh_g = sb("tanh_g", [P, 2])
        bo_row = sb("bo_row", [1, D])
        bo_gated = sb("bo_gated", [1, D])
        area = sb("area", [P, 6, 1024])
        wq_pair, wk_diag, wv_diag, wo_pair, a_full = (
            area[:, i, :].rearrange("p (h n) -> p h n", h=PAIRS) for i in range(5))
        probs_t = area[:, 0:2, :].rearrange("p a n -> p (a n)").rearrange("p (k h n) -> p k h n", k=4, h=4)
        u_norm = area[:, 2:4, :].rearrange("p a (h q d) -> p a h q d", h=PAIRS, q=2)
        u_t = area[:, 4:6, :].rearrange("p a (h n) -> p a h n", h=PAIRS)
        silu_g, gated = (area[:, i, :].rearrange("p (a n) -> p a n", a=2) for i in range(2))
        hid = area[:, 2:4, :].rearrange("p a n -> p (a n)")[:, 0:HIDS * CT].rearrange("p (a n) -> p a n", a=HIDS)
        result, x2t, y_t = area[:, 3, CT:2 * CT], area[:, 4, 0:CT], area[:, 4, CT:2 * CT]
        a_hi = sb("a_hi", [P, PAIRS, P], F32R)
        a_lo = sb("a_lo", [P, PAIRS, P], F32R)
        c_pair = sb("c_pair", [P, PAIRS, D])
        ctx_keys = sb("ctx_keys", [P, CB, CD + 1])
        ctx_raw = sb("ctx_raw", [P, CB, P])
        diag_hi = sb("diag_hi", [P, CB, 2, P], F32R)
        diag_lo = sb("diag_lo", [P, CB, 2, P], F32R)
        bn6 = sb("bn6", [P, CB, 6])
        mean_var = sb("mean_var", [P, CB, 2])
        var_eps = sb("var_eps", [P, CB])
        half_var = sb("half_var", [P, CB])
        rsqrt_bits = sb("rsqrt_bits", [P, CB])
        guess = sb("guess", [P, NEWTON_STEPS, CB])
        newton = sb("newton", [P, 2, CB])
        rstd = sb("rstd", [P, CB])
        xn = sb("xn", [P, CB, D])
        xnt_hi = sb("xnt_hi", [P, CT], F32R)
        xnt_lo = sb("xnt_lo", [P, CT], F32R)
        halves = sb("halves", [P, 2, 2 * PAIRS * 2 * P], F32R)
        g_hi, g_lo = (halves[:, i, :].rearrange("p (r h n) -> p r h n", r=2, h=PAIRS) for i in range(2))
        hid_hi, hid_lo = (halves[:, i, 0:SLOTS * CT].rearrange("p (s n) -> p s n", s=SLOTS) for i in range(2))
        row_max = sb("row_max", [P, 2, HEADS])
        max_t = sb("max_t", [HEADS, 2, P], F32R)
        max_row = sb("max_row", [1, 2, HEADS, P], F32R)
        inv_sum = sb("inv_sum", [P, 4, 4])
        w_raw = sb("w_raw", [P, 2, WSTEP])
        w_hi = sb("w_hi", [P, WCOLS], F32R)
        w_lo = sb("w_lo", [P, WCOLS], F32R)
        router_w = sb("router_w", [P, NE])
        bias_bc = sb("bias_bc", [P, NE])
        expand = sb("expand", [3 * NE, NE // 2, P], BF16)
        x2t_hi = sb("x2t_hi", [P, 2, CT], F32R)
        x2t_lo = sb("x2t_lo", [P, 2, CT], F32R)
        logits = sb("logits", [P, CB * NE])
        logits_low = sb("logits_low", [P, CB * NE])
        tanh_half = sb("tanh_half", [P, CB * NE])
        silu_low = sb("silu_low", [P, CB * NE])
        sig = sb("sig", [P, 5, CB * NE])
        score = sb("score", [P, CB, NE])
        choice = sb("choice", [P, CB, NE])
        top_in_group = sb("top_in_group", [P, CB, GROUPS, 8])
        group_score = sb("group_score", [P, CB, GROUPS + 6])
        group_top = sb("group_top", [P, CB, 8])
        group_pick = sb("group_pick", [P, CB, 8])
        group_left = sb("group_left", [P, CB, GROUPS + 6])
        group_mask = sb("group_mask", [P, CB, GROUPS])
        masked = sb("masked", [P, CB, NE])
        expert_top = sb("expert_top", [P, CB, 8])
        expert_left = sb("expert_left", [P, CB, NE])
        weight = sb("weight", [P, 2, CB, NE])
        weight_sum = sb("weight_sum", [P, 2, CB])
        weight_inv = sb("weight_inv", [P, CB])
        rest = sb("rest", [P, 2, CB, NE])
        w_parts = sb("w_parts", [P, CB, 3, NE], BF16)
        w_parts_t = sb("w_parts_t", [3 * NE, 2, CT], BF16)

        bank = [stack.enter_context(nc.psum_tensor(f"bank{i}", [P, 512], F32)) for i in range(8)]
        scores_ps, st_ps, u_ps, ut_ps, small_ps = bank[0:2], bank[2:4], bank[4:6], bank[6], bank[7]
        gate_ps, up_ps, wbc_ps, y_ps, misc_ps = bank[0:2], bank[2:4], bank[4:6], bank[6], bank[7]

        x_in = [sem("x_in0"), sem("x_in1")]
        weights_in, small_in = sem("weights_in"), sem("small_in")
        keys_in = [sem(f"keys_in{b}") for b in range(CB)]
        raw_in = [sem(f"raw_in{b}") for b in range(CB)]
        wraw_in = [sem("wraw_in0"), sem("wraw_in1")]
        maxrow_in = [sem("maxrow_in0"), sem("maxrow_in1")]
        result_free = sem("result_free")
        zeroed, const_step, const_ready = sem("zeroed"), sem("const_step"), sem("const_ready")
        tanh_ready, bo_ready = sem("tanh_ready"), sem("bo_ready")
        fold_done, a_ready, ahi_ready, alo_ready, c_ready = (
            sem("fold_done"), sem("a_ready"), sem("ahi_ready"), sem("alo_ready"), sem("c_ready"))
        ln_step, xn_ready = sem("ln_step"), sem("xn_ready")
        xt_done, xhi_ready, xlo_ready = sem("xt_done"), sem("xhi_ready"), sem("xlo_ready")
        g_done, ghi_ready, glo_ready = sem("g_done"), sem("ghi_ready"), sem("glo_ready")
        diaghi_ready, diag_ready = sem("diaghi_ready"), sem("diag_ready")
        waits_passed, loads_begun = sem("waits_passed"), sem("loads_begun")
        wsplit_hi, wsplit_ready = sem("wsplit_hi"), sem("wsplit_ready")
        smax_done, max_ready = sem("smax_done"), sem("max_ready")
        maxt_done, maxt_ready = sem("maxt_done"), sem("maxt_ready")
        st_done, exp_ready = sem("st_done"), sem("exp_ready")
        u_done, inv_ready, norm_ready = sem("u_done"), sem("inv_ready"), sem("norm_ready")
        ut_done, ut_ready = sem("ut_done"), sem("ut_ready")
        attn_done, x2_ready = sem("attn_done"), sem("x2_ready")
        x2t_ready, x2hi_ready, x2lo_ready = sem("x2t_ready"), sem("x2hi_ready"), sem("x2lo_ready")
        logits_done, logits_ready, sig_ready = sem("logits_done"), sem("logits_ready"), sem("sig_ready")
        route_step, parts_ready = sem("route_step"), sem("parts_ready")
        wt_done, wt_ready = sem("wt_done"), sem("wt_ready")
        gate_done, up_done, wbc_done = sem("gate_done"), sem("up_done"), sem("wbc_done")
        silu_ready, gated_ready = sem("silu_ready"), sem("gated_ready")
        hid_ready, hidhi_ready, hidlo_ready = sem("hid_ready"), sem("hidhi_ready"), sem("hidlo_ready")
        down_done, yt_ready = sem("down_done"), sem("yt_ready")
        y_done, result_ready = sem("y_done"), sem("result_ready")

        def wait(eng, s, value):
            if isinstance(value, int) and value <= 0:
                return
            eng.wait_ge(s, value)

        x_dram = x.rearrange("b n d -> n b d")
        out_dram = out.rearrange("b n d -> n b d")

        def group(k):
            return slice(4 * (k // 2), 4 * (k // 2) + 4), k % 2

        def in_chunks(eng, body):
            body(0, True, False)
            with eng.Fori(1, NCH - 1) as c:
                body(c, False, False)
            body(NCH - 1, False, True)

        def in_chunk_pairs(eng, body):
            body(0, 0, True, False)
            with eng.Fori(0, NCH // 2 - 1) as i:
                body(2 * i + 1, 1, False, False)
                body(2 * i + 2, 0, False, False)
            body(NCH - 1, (NCH - 1) % 2, False, True)

        def free_of(slots, c, u):
            if u >= slots:
                return UNITS * c + u - slots + 1
            before = max(v for v in range(UNITS) if v % slots == u)
            return UNITS * c - UNITS + before + 1

        block = stack.enter_context(nc.Block())

        @block.sync
        def _(sp):
            def wait_first(s, value):
                wait(sp, s, value)
                sp.sem_inc(loads_begun, 1)

            def load_keys(b, t):
                sp.dma_start(ctx_keys[:, b, 0:CD], ctx_nat[:, bass.ds(t, 1), :].rearrange("m a d -> m (a d)"))\
                    .then_inc(keys_in[b], 16)

            def load_raw(b, tokens):
                for q in range(2):
                    sp.dma_start(ctx_raw[q * CD:q * CD + CD, b, :], ctx_t[:, bass.ds(tokens, P)])\
                        .then_inc(raw_in[b], 16)

            def load_weights(slot, cols):
                sp.dma_start(w_raw[:, slot, :], experts[:, bass.ds(cols, WSTEP)]).then_inc(wraw_in[slot], 16)

            def load_max_row(t, parity, before):
                wait_first(maxt_ready, t + 1)
                wait_first(st_done, 4 * before + 4)
                sp.dma_start(raw(max_row[0:1, parity, :, :]), raw(max_t[:, parity, :])).then_inc(maxrow_in[parity], 16)

            sp.dma_start(x_sb[:, 0:CB, :], x_dram[:, 0:CB, :]).then_inc(x_in[0], 16)
            for n, g in enumerate((g_xattn, g_ffn)):
                sp.dma_start(gates[:, n:n + 1], g.rearrange("(a n) -> a n", a=1).broadcast_to([P, 1]))\
                    .then_inc(small_in, 16)
            sp.dma_start(bo_row[:], bo.rearrange("(a n) -> a n", a=1)).then_inc(small_in, 16)
            sp.dma_start(bias_bc[:], router_bias.rearrange("(a n) -> a n", a=1).broadcast_to([P, NE]))\
                .then_inc(small_in, 16)
            sp.dma_start(router_w[:], router_t).then_inc(small_in, 16)
            sp.dma_start(wq_pair, wq_t.rearrange("(p r) n -> r p n", r=P)).then_inc(weights_in, 16)
            sp.dma_start(wo_pair, wo.rearrange("(p r) n -> r p n", r=P)).then_inc(weights_in, 16)
            sp.wait_ge(zeroed, 2)
            for q in range(2):
                rows = slice(q * HD, q * HD + HD)
                for diag, w in ((wk_diag, wk_t), (wv_diag, wv_t)):
                    sp.dma_start(diag[rows, :, q * CD:q * CD + CD],
                                 w.rearrange("(p q r) n -> q r p n", q=2, r=HD)[q]).then_inc(weights_in, 16)
            for b in range(CB):
                load_raw(b, b * P)
            for b in range(CB - 1):
                load_keys(b, b)
            sp.dma_start(x_sb[:, CB:NB, :], x_dram[:, CB:NB, :]).then_inc(x_in[1], 16)
            for slot in range(2):
                load_weights(slot, slot * WSTEP)
            load_max_row(0, 0, -2)

            def attention(c, first, last):
                for b in range(CB):
                    t = CB * c + b
                    if not last:
                        wait_first(diag_ready, 2 * t + 2)
                        load_raw(b, (t + CB) * P)
                    if not (last and b >= 2):
                        wait_first(wsplit_ready, t + 1)
                        load_weights(b % 2, (t + 2) * WSTEP)
                    if not (last and b == CB - 1):
                        load_max_row(t + 1, (b + 1) % 2, t - 1)
                    if not (last and b > 0):
                        wait_first(u_done, 4 * t)
                        load_keys((b - 1) % CB, t - 1 + CB)

            in_chunks(sp, attention)

            sp.sem_inc(result_free, 16)
            with sp.Fori(0, NCH) as c:
                wait_first(result_ready, c + 1)
                sp.dma_start(out_dram[:, bass.ds(c * CB, CB), :], result.rearrange("p (b d) -> p b d", b=CB))\
                    .then_inc(result_free, 16)
            sp.wait_ge(result_free, 16 * NCH + 16)

        @block.gpsimd
        def _(pool):
            nc.gpsimd.memset(wk_diag, 0.0).then_inc(zeroed, 1)
            nc.gpsimd.memset(wv_diag, 0.0).then_inc(zeroed, 1)
            nc.gpsimd.memset(ones_col[:], 1.0).then_inc(const_step, 1)
            nc.gpsimd.memset(ident[:], 0.0).then_inc(const_step, 1)
            nc.gpsimd.memset(ident_bf[:], 0.0).then_inc(const_step, 1)
            nc.gpsimd.memset(expand[:], 0.0).then_inc(const_step, 1)
            nc.gpsimd.memset(raw(neg_ones[:]), -1.0).then_inc(const_ready, 1)
            nc.gpsimd.memset(ones_row[:], 1.0).then_inc(const_ready, 1)
            nc.gpsimd.memset(ctx_keys[:, :, CD:CD + 1], 1.0).then_inc(const_ready, 1)
            nc.gpsimd.memset(group_score[:], LOWEST).then_inc(const_ready, 1)
            nc.gpsimd.memset(group_pick[:], LOWEST).then_inc(const_ready, 1)
            pool.wait_ge(const_step, 4)
            for m in (ident, ident_bf):
                nc.gpsimd.affine_select(out=m[:], in_=m[:], compare_op=ALU.not_equal, fill=1.0, base=0,
                                        pattern=[[-1, P]], channel_multiplier=1).then_inc(const_ready, 1)
            nc.gpsimd.memset(raw(diag_hi[:]), 0.0).then_inc(zeroed, 1)
            nc.gpsimd.memset(raw(diag_lo[:]), 0.0).then_inc(zeroed, 1)

            def split_context(b, t, c):
                pool.wait_ge(raw_in[b], 32 * c + 32)
                wait(pool, wsplit_ready, t - CB + 1)
                wait(pool, st_done, 4 * (t - CB) + 4)
                for q in range(2):
                    rows = slice(q * CD, q * CD + CD)
                    nc.gpsimd.tensor_tensor(diag_hi[rows, b, q, :], ctx_raw[rows, b, :],
                                            ones_col[rows, :].broadcast_to([CD, P]), ALU.mult)\
                        .then_inc(diaghi_ready, 1)
                pool.wait_ge(diaghi_ready, 2 * t + 2)
                for q in range(2):
                    rows = slice(q * CD, q * CD + CD)
                    nc.gpsimd.tensor_tensor(diag_lo[rows, b, q, :], ctx_raw[rows, b, :],
                                            raw(diag_hi[rows, b, q, :]), ALU.subtract).then_inc(diag_ready, 1)

            def split_weights(slot, t, nth, contexts):
                cols = bass.ds(t * WSTEP, WSTEP)
                pool.wait_ge(wraw_in[slot], 16 * nth + 16)
                pool.wait_ge(diag_ready, contexts)
                nc.gpsimd.tensor_tensor(w_hi[:, cols], w_raw[:, slot, :], ones_col[:].broadcast_to([P, WSTEP]),
                                        ALU.mult).then_inc(wsplit_hi, 1)
                pool.wait_ge(wsplit_hi, t + 1)
                nc.gpsimd.tensor_tensor(w_lo[:, cols], w_raw[:, slot, :], raw(w_hi[:, cols]), ALU.subtract)\
                    .then_inc(wsplit_ready, 1)

            pool.wait_ge(zeroed, 4)
            for b in range(CB):
                split_context(b, b, 0)
            pool.wait_ge(diag_ready, 2 * CB)
            for part in range(3):
                rows = expand[part * NE:(part + 1) * NE].rearrange("j u (e i) -> j u e i", e=2)
                nc.gpsimd.affine_select(out=rows, in_=rows, compare_op=ALU.not_equal, fill=1.0, base=0,
                                        pattern=[[-2, NE // 2], [-1, 2], [0, EI]], channel_multiplier=1)\
                    .then_inc(const_ready, 1)
            pool.wait_ge(const_ready, 10)

            def attention(c, first, last):
                for b in range(CB):
                    t = CB * c + b
                    split_weights(b % 2, t, 2 * c + b // 2, 2 * NB if last else 2 * (t + CB))
                    if not last:
                        split_context(b, t + CB, c + 1)

            in_chunks(pool, attention)

            def experts_low(c):
                for u in range(UNITS):
                    n = UNITS * c + u
                    pool.wait_ge(hidhi_ready, n + 1)
                    wait(pool, down_done, free_of(SLOTS, c, u))
                    nc.gpsimd.tensor_tensor(hid_lo[:, u % SLOTS, :], hid[:, u % HIDS, :], raw(hid_hi[:, u % SLOTS, :]),
                                            ALU.subtract).then_inc(hidlo_ready, 1)

            experts_low(0)
            with pool.Fori(1, NCH) as c:
                experts_low(c)

        @block.scalar
        def _(act):
            def xt_high(i):
                act.wait_ge(xt_done, i + 1)
                wait(act, g_done, 8 * i)
                nc.scalar.activation(xnt_hi[:], ut_ps[:], ACT.Copy).then_inc(xhi_ready, 1)

            def g_high(g, ring):
                for j in range(4):
                    act.wait_ge(g_done, 4 * g + j + 1)
                    wait(act, st_done, 8 * g - 8)
                    nc.scalar.activation(g_hi[:, ring, 2 * j:2 * j + 2, :],
                                         bank[j][:].rearrange("p (h n) -> p h n", h=2), ACT.Copy)\
                        .then_inc(ghi_ready, 1)

            def max_out(t, parity, loads_before):
                act.wait_ge(maxt_done, t + 1)
                wait(act, maxrow_in[parity], 16 * loads_before)
                nc.scalar.activation(max_t[:, parity, :], small_ps[0:HEADS, 0:P], ACT.Copy).then_inc(maxt_ready, 1)

            def ut_out(t, parity, r):
                act.wait_ge(ut_done, 2 * t + r + 1)
                wait(act, attn_done, t - 1)
                nc.scalar.activation(u_t[:, parity, 4 * r:4 * r + 4, :],
                                     ut_ps[:].rearrange("p (h n) -> p h n", h=4), ACT.Copy).then_inc(ut_ready, 1)

            act.wait_ge(small_in, 16 * 5)
            nc.scalar.activation(tanh_g[:], gates[:], ACT.Tanh).then_inc(tanh_ready, 1)
            act.wait_ge(tanh_ready, 1)
            nc.scalar.activation(bo_gated[:], bo_row[:], ACT.Copy, scale=tanh_g[0:1, 0:1]).then_inc(bo_ready, 1)
            for i in range(2):
                act.wait_ge(fold_done, i + 1)
                half = slice(4 * i, 4 * i + 4)
                nc.scalar.activation(a_full[:, half, :], bank[i][:].rearrange("p (h n) -> p h n", h=4), ACT.Copy,
                                     scale=SCALE).then_inc(a_ready, 1)
                act.wait_ge(a_ready, i + 1)
                nc.scalar.activation(a_hi[:, half, :], a_full[:, half, :], ACT.Copy).then_inc(ahi_ready, 1)
            xt_high(0)
            for i in range(2):
                act.wait_ge(fold_done, i + 3)
                nc.scalar.activation(c_pair[:, 4 * i:4 * i + 4, :], bank[2 + i][:].rearrange("p (h n) -> p h n", h=4),
                                     ACT.Copy, scale=tanh_g[:, 0:1]).then_inc(c_ready, 1)
            for ring in range(2):
                g_high(ring, ring)
            max_out(0, 0, 0)

            def attention(c, first, last):
                for b in range(CB):
                    t = CB * c + b
                    for k in range(4):
                        if k == 2 and not (last and b == CB - 1):
                            max_out(t + 1, (b + 1) % 2, 2 * c + (b - 1) // 2 + 1)
                        if b == 1 and k == 3 and not last:
                            xt_high(c + 1)
                        act.wait_ge(st_done, 4 * t + k + 1)
                        wait(act, u_done, 4 * t + k - 3)
                        nc.scalar.activation(probs_t[:, k, :, :],
                                             st_ps[k % 2][:].rearrange("p (h n) -> p h n", h=4), ACT.Exp)\
                            .then_inc(exp_ready, 1)
                        if k == 2 and not (first and b == 0):
                            ut_out(t - 1, (b - 1) % 2, 1)
                        if k == 3:
                            ut_out(t, b % 2, 0)
                    if b % 2 == 1 and not last:
                        g_high(2 * c + 2 + b // 2, b // 2)

            in_chunks(act, attention)
            ut_out(NB - 1, (NB - 1) % 2, 1)

            def x2t_out(c):
                act.wait_ge(xt_done, NCH + c + 1)
                nc.scalar.activation(x2t, misc_ps[:], ACT.Copy).then_inc(x2t_ready, 1)

            def x2t_high(c, parity):
                act.wait_ge(x2t_ready, c + 1)
                wait(act, up_done, UNITS * (c - 1))
                nc.scalar.activation(x2t_hi[:, parity, :], x2t, ACT.Copy).then_inc(x2hi_ready, 1)

            def logits_out(c):
                act.wait_ge(logits_done, c + 1)
                nc.scalar.activation(logits[:], misc_ps[:, 0:CB * NE], ACT.Copy).then_inc(logits_ready, 1)

            def sigmoids(c):
                act.wait_ge(logits_ready, c + 1)
                nc.scalar.activation(tanh_half[:], logits[:], ACT.Tanh, scale=0.5).then_inc(sig_ready, 1)
                act.wait_ge(route_step, ROUTE_STEPS * c + 1)
                nc.scalar.activation(silu_low[:], logits_low[:], ACT.Silu).then_inc(sig_ready, 1)

            def weights_out(c, parity):
                act.wait_ge(wt_done, c + 1)
                wait(act, wbc_done, (UNITS - 1) * (c - 1))
                nc.scalar.activation(w_parts_t[:, parity, :], misc_ps[:].bitcast(BF16)[0:3 * NE, 0:CT], ACT.Copy)\
                    .then_inc(wt_ready, 1)

            def hidden_high(c, u):
                act.wait_ge(hid_ready, UNITS * c + u + 1)
                wait(act, down_done, free_of(SLOTS, c, u))
                nc.scalar.activation(hid_hi[:, u % SLOTS, :], hid[:, u % HIDS, :], ACT.Copy).then_inc(hidhi_ready, 1)

            def y_out(c):
                act.wait_ge(down_done, UNITS * (c + 1))
                nc.scalar.activation(y_t, y_ps[:], ACT.Copy).then_inc(yt_ready, 1)

            def experts_of(c, parity, first, last):
                for u in range(UNITS):
                    act.wait_ge(gate_done, UNITS * c + u + 1)
                    wait(act, gated_ready, free_of(2, c, u))
                    nc.scalar.activation(silu_g[:, u % 2, :], gate_ps[u % 2][:], ACT.Silu).then_inc(silu_ready, 1)
                    if u >= 2:
                        hidden_high(c, u - 2)
                    elif not first:
                        hidden_high(c - 1, UNITS - 2 + u)
                    if u == 0:
                        weights_out(c, parity)
                    if u == LAG and not first:
                        y_out(c - 1)
                    if not last:
                        if u == 6:
                            x2t_out(c + 1)
                        if u == 7:
                            x2t_high(c + 1, 1 - parity)
                        if u == 8:
                            logits_out(c + 1)
                        if u == 9:
                            sigmoids(c + 1)

            x2t_out(0)
            x2t_high(0, 0)
            logits_out(0)
            sigmoids(0)
            in_chunk_pairs(act, experts_of)
            for u in (UNITS - 2, UNITS - 1):
                hidden_high(NCH - 1, u)
            y_out(NCH - 1)

        @block.vector
        def _(dve):
            def wait_first(s, value):
                dve.wait_ge(s, value)
                dve.sem_inc(waits_passed, 1)

            def ln_level(n, t, level):
                base = LN_STEPS * n
                i, newton_op = divmod(level - 5, 3)
                if level == 0:
                    for b in range(CB):
                        nc.vector.bn_stats(bn6[:, b, :], x_sb[:, bass.ds(t + b, 1), :].rearrange("p a d -> p (a d)"))\
                            .then_inc(ln_step, 1)
                elif level == 1:
                    wait_first(ln_step, base + CB)
                    for b in range(CB):
                        nc.vector.bn_aggr(mean_var[:, b, :], bn6[:, b, :]).then_inc(ln_step, 1)
                elif level == 2:
                    dve.wait_ge(ln_step, base + 2 * CB)
                    nc.vector.tensor_scalar(var_eps[:], mean_var[:, :, 1], EPS, None, ALU.add).then_inc(ln_step, 1)
                    nc.vector.tensor_scalar(half_var[:], mean_var[:, :, 1], EPS, -0.5, ALU.add, ALU.mult)\
                        .then_inc(ln_step, 1)
                elif level == 3:
                    dve.wait_ge(ln_step, base + 2 * CB + 2)
                    nc.vector.tensor_scalar(rsqrt_bits[:].bitcast(I32), var_eps[:].bitcast(I32), 1, 0x7fffffff,
                                            ALU.logical_shift_right, ALU.bitwise_xor).then_inc(ln_step, 1)
                elif level == 4:
                    dve.wait_ge(ln_step, base + 2 * CB + 3)
                    nc.vector.tensor_scalar(guess[:, 0, :], rsqrt_bits[:], GUESS_SCALE, None, ALU.mult)\
                        .then_inc(ln_step, 1)
                elif level == LN_LEVELS - 1:
                    dve.wait_ge(ln_step, base + LN_STEPS)
                    wait(dve, xt_done, n)
                    for b in range(CB):
                        nc.vector.tensor_scalar(xn[:, b, :], x_sb[:, bass.ds(t + b, 1), :].rearrange("p a d -> p (a d)"),
                                                mean_var[:, b, 0:1], rstd[:, b:b + 1], ALU.subtract, ALU.mult)\
                            .then_inc(xn_ready, 1)
                else:
                    r, better = guess[:, i, :], rstd[:] if i == NEWTON_STEPS - 1 else guess[:, i + 1, :]
                    dve.wait_ge(ln_step, base + 2 * CB + 4 + 3 * i + newton_op)
                    if newton_op == 0:
                        ins = nc.vector.tensor_tensor(newton[:, 0, :], r, r, ALU.mult)
                    elif newton_op == 1:
                        ins = nc.vector.tensor_tensor(newton[:, 1, :], newton[:, 0, :], half_var[:], ALU.mult)
                    else:
                        ins = nc.vector.scalar_tensor_tensor(better, newton[:, 1, :], 1.5, r, ALU.add, ALU.mult)
                    ins.then_inc(ln_step, 1)

            def layer_norm(n, t):
                for level in range(LN_LEVELS):
                    ln_level(n, t, level)

            def xt_low(i):
                dve.wait_ge(xhi_ready, i + 1)
                nc.vector.tensor_tensor(xnt_lo[:], ut_ps[:], raw(xnt_hi[:]), ALU.subtract).then_inc(xlo_ready, 1)

            def g_low(g, ring):
                for j in range(4):
                    dve.wait_ge(ghi_ready, 4 * g + j + 1)
                    nc.vector.tensor_tensor(g_lo[:, ring, 2 * j:2 * j + 2, :],
                                            bank[j][:].rearrange("p (h n) -> p h n", h=2),
                                            raw(g_hi[:, ring, 2 * j:2 * j + 2, :]), ALU.subtract)\
                        .then_inc(glo_ready, 1)

            def take_max(t, parity, k):
                dve.wait_ge(smax_done, 4 * t + k + 1)
                wait(dve, maxt_done, t - 1)
                nc.vector.tensor_reduce(row_max[:, parity, 4 * k:4 * k + 4],
                                        scores_ps[k % 2][:].rearrange("p (h m) -> p h m", h=4), AX_X, ALU.max)\
                    .then_inc(max_ready, 1)

            def normalise(t, parity, k):
                pairs, q = group(k)
                u = u_ps[k % 2][:, 0:4 * (CD + 1)].rearrange("p (h d) -> p h d", h=4)
                dve.wait_ge(u_done, 4 * t + k + 1)
                wait(dve, inv_ready, 4 * t + k - 3)
                nc.vector.reciprocal(inv_sum[:, k, :], u[:, :, CD]).then_inc(inv_ready, 1)
                dve.wait_ge(inv_ready, 4 * t + k + 1)
                wait(dve, ut_done, 2 * (t - 2) + k // 2 + 1)
                nc.vector.tensor_tensor(u_norm[:, parity, pairs, q, :], u[:, :, 0:CD],
                                        inv_sum[:, k, :].unsqueeze(2).broadcast_to([P, 4, CD]), ALU.mult)\
                    .then_inc(norm_ready, 1)

            def residual(t):
                dve.wait_ge(attn_done, t + 1)
                tile = x_sb[:, bass.ds(t, 1), :].rearrange("p a d -> p (a d)")
                nc.vector.tensor_tensor(tile, small_ps[:, D:2 * D], tile, ALU.add).then_inc(x2_ready, 1)

            dve.wait_ge(x_in[0], 16)
            layer_norm(0, 0)
            for i in range(2):
                dve.wait_ge(ahi_ready, i + 1)
                half = slice(4 * i, 4 * i + 4)
                nc.vector.tensor_tensor(a_lo[:, half, :], a_full[:, half, :], raw(a_hi[:, half, :]), ALU.subtract)\
                    .then_inc(alo_ready, 1)
            xt_low(0)
            for ring in range(2):
                g_low(ring, ring)
            dve.wait_ge(x_in[1], 16)
            for b in range(2):
                for k in range(4):
                    take_max(b, b, k)

            def attention(c, first, last):
                for b in range(CB):
                    t = CB * c + b
                    for k in range(4):
                        if not (last and b >= 2):
                            take_max(t + 2, b % 2, k)
                        if k > 0:
                            normalise(t, b % 2, k - 1)
                        elif not (first and b == 0):
                            normalise(t - 1, (b - 1) % 2, 3)
                        if k == 0 and not (first and b < 2):
                            residual(t - 2)
                        if 4 * b + k < LN_SPREAD and not last:
                            for level in range((4 * b + k) * LN_LEVELS // LN_SPREAD, (4 * b + k + 1) * LN_LEVELS // LN_SPREAD):
                                ln_level(c + 1, t - b + CB, level)
                        if b == 1 and k == 3 and not last:
                            xt_low(c + 1)
                    if b % 2 == 1 and not last:
                        g_low(2 * c + 2 + b // 2, b // 2)

            in_chunks(dve, attention)
            normalise(NB - 1, (NB - 1) % 2, 3)
            residual(NB - 2)
            residual(NB - 1)

            def step(ins):
                ins.then_inc(route_step, 1)
                counted[0] += 1

            def so_far(c, alone=False):
                (wait_first if alone else dve.wait_ge)(route_step, ROUTE_STEPS * c + counted[0])

            counted = [0]

            def logits_below(c):
                counted[0] = 0
                dve.wait_ge(logits_ready, c + 1)
                step(nc.vector.tensor_scalar(logits_low[:], logits[:], -1.0, None, ALU.min))

            low_inv, high, low, rise, risen = (sig[:, i, :] for i in range(5))

            def sigmoid_high(c):
                dve.wait_ge(sig_ready, 2 * c + 2)
                step(nc.vector.reciprocal(low_inv, logits_low[:]))
                step(nc.vector.tensor_scalar(high, tanh_half[:], 0.5, 0.5, ALU.mult, ALU.add))

            def sigmoid_low(c):
                so_far(c)
                step(nc.vector.tensor_tensor(low, silu_low[:], low_inv, ALU.mult))

            def sigmoid_rise(c):
                so_far(c)
                step(nc.vector.tensor_tensor(rise, high, low, ALU.subtract))

            def sigmoid_risen(c):
                so_far(c)
                step(nc.vector.scalar_tensor_tensor(risen, logits[:], -1.0, rise, ALU.is_gt, ALU.mult))

            def scores_of(c):
                so_far(c)
                step(nc.vector.tensor_tensor(flat(score[:], 3), low, risen, ALU.add))

            def choices(c):
                so_far(c)
                step(nc.vector.tensor_tensor(choice[:], score[:], bias_bc[:].unsqueeze(1).broadcast_to([P, CB, NE]),
                                             ALU.add))

            def best_in_groups(c):
                so_far(c, alone=True)
                for i in range(CB):
                    for g in range(GROUPS):
                        step(nc.vector.max(top_in_group[:, i, g, :], choice[:, i, g * GE:(g + 1) * GE]))

            def group_scores(c):
                so_far(c)
                step(nc.vector.tensor_tensor(group_score[:, :, 0:GROUPS], top_in_group[:, :, :, 0],
                                             top_in_group[:, :, :, 1], ALU.add))

            def best_groups(c):
                so_far(c, alone=True)
                for i in range(CB):
                    step(nc.vector.max(group_top[:, i, :], group_score[:, i, :]))

            def take_groups(c):
                so_far(c)
                step(nc.vector.tensor_copy(group_pick[:, :, 0:GROUPS_TAKEN], group_top[:, :, 0:GROUPS_TAKEN]))

            def mark_groups(c):
                so_far(c, alone=True)
                for i in range(CB):
                    step(nc.vector.match_replace(group_left[:, i, :], group_pick[:, i, :], group_score[:, i, :], PICKED))

            def mask_groups(c):
                so_far(c)
                step(nc.vector.tensor_scalar(group_mask[:], group_left[:, :, 0:GROUPS], PICKED, None, ALU.is_equal))

            def mask_experts(c):
                so_far(c)
                step(nc.vector.tensor_tensor(
                    flat(masked[:], 3).rearrange("p (b e) -> p b e", e=GE),
                    flat(choice[:], 3).rearrange("p (b e) -> p b e", e=GE),
                    flat(group_mask[:], 3).unsqueeze(2).broadcast_to([P, CB * GROUPS, GE]), ALU.mult))

            def best_experts(c):
                so_far(c, alone=True)
                for i in range(CB):
                    step(nc.vector.max(expert_top[:, i, :], masked[:, i, :]))

            def mark_experts(c):
                so_far(c, alone=True)
                for i in range(CB):
                    step(nc.vector.match_replace(expert_left[:, i, :], expert_top[:, i, :], masked[:, i, :], PICKED))

            def picked_scores(c):
                so_far(c)
                step(nc.vector.scalar_tensor_tensor(flat(weight[:, 0], 3), flat(expert_left[:], 3), PICKED,
                                                    flat(score[:], 3), ALU.is_equal, ALU.mult))

            def picked_sum(c):
                so_far(c)
                step(nc.vector.tensor_reduce(weight_sum[:, 0, :], weight[:, 0], AX_X, ALU.add))

            def picked_guard(c):
                so_far(c)
                step(nc.vector.tensor_scalar(weight_sum[:, 1, :], weight_sum[:, 0, :], 1e-20, None, ALU.add))

            def picked_inverse(c):
                so_far(c)
                step(nc.vector.reciprocal(weight_inv[:], weight_sum[:, 1, :]))

            def weights_of(c):
                so_far(c)
                step(nc.vector.scalar_tensor_tensor(weight[:, 1], weight[:, 0], ROUTED_SCALING,
                                                    weight_inv[:].unsqueeze(2).broadcast_to([P, CB, NE]),
                                                    ALU.mult, ALU.mult))

            def first_part(c):
                so_far(c)
                wait(dve, wt_done, c)
                step(nc.vector.tensor_copy(w_parts[:, :, 0, :], weight[:, 1]))

            def first_rest(c):
                so_far(c)
                step(nc.vector.tensor_tensor(rest[:, 0], weight[:, 1], w_parts[:, :, 0, :], ALU.subtract))

            def second_part(c):
                so_far(c)
                step(nc.vector.tensor_copy(w_parts[:, :, 1, :], rest[:, 0]))

            def second_rest(c):
                so_far(c)
                step(nc.vector.tensor_tensor(rest[:, 1], rest[:, 0], w_parts[:, :, 1, :], ALU.subtract))

            def third_part(c):
                so_far(c)
                nc.vector.tensor_copy(w_parts[:, :, 2, :], rest[:, 1]).then_inc(parts_ready, 1)
                assert counted[0] == ROUTE_STEPS

            route_levels = (
                logits_below, sigmoid_high, sigmoid_low, sigmoid_rise, sigmoid_risen, scores_of, choices,
                best_in_groups, group_scores, best_groups, take_groups, mark_groups, mask_groups, mask_experts,
                best_experts, mark_experts, picked_scores, picked_sum, picked_guard, picked_inverse, weights_of,
                first_part, first_rest, second_part, second_rest, third_part)

            def levels_at(c, u, place, last):
                if last:
                    return
                if u <= 4:
                    for level in ((3 * u,), (3 * u + 1, 3 * u + 2))[place]:
                        ln_level(NCH + c + 1, CB * (c + 1), level)
                if u == 8 and place == 1:
                    route_levels[0](c + 1)
                if u >= 10:
                    at = 1 + 4 * (u - 10) + 2 * place
                    for level in route_levels[at:at + 2]:
                        level(c + 1)

            def x2t_low(c, parity):
                dve.wait_ge(x2hi_ready, c + 1)
                nc.vector.tensor_tensor(x2t_lo[:, parity, :], x2t, raw(x2t_hi[:, parity, :]), ALU.subtract)\
                    .then_inc(x2lo_ready, 1)

            def result_of(c):
                dve.wait_ge(y_done, c + 1)
                dve.wait_ge(result_free, 16 * c + 16)
                nc.vector.scalar_tensor_tensor(
                    result, misc_ps[:], tanh_g[:, 1:2],
                    x_sb[:, bass.ds(CB * c, CB), :].rearrange("p b d -> p (b d)"), ALU.mult, ALU.add)\
                    .then_inc(result_ready, 1)

            def gate_up(c, u):
                n = UNITS * c + u
                dve.wait_ge(silu_ready, n + 1)
                dve.wait_ge(up_done, n + 1)
                wait(dve, hid_ready, free_of(2, c, u))
                nc.vector.tensor_tensor(gated[:, u % 2, :], silu_g[:, u % 2, :], up_ps[u % 2][:], ALU.mult)\
                    .then_inc(gated_ready, 1)

            def weigh_hidden(c, u):
                dve.wait_ge(gated_ready, UNITS * c + u + 1)
                wait(dve, hidlo_ready, free_of(HIDS, c, u))
                if u == 0:
                    nc.vector.tensor_copy(hid[:, u % HIDS, :], gated[:, u % 2, :]).then_inc(hid_ready, 1)
                else:
                    dve.wait_ge(wbc_done, (UNITS - 1) * c + u)
                    nc.vector.tensor_tensor(hid[:, u % HIDS, :], gated[:, u % 2, :], wbc_ps[u % 2][:], ALU.mult)\
                        .then_inc(hid_ready, 1)

            def experts_of(c, parity, first, last):
                for u in range(UNITS):
                    gate_up(c, u)
                    levels_at(c, u, 0, last)
                    if u > 0:
                        weigh_hidden(c, u - 1)
                    levels_at(c, u, 1, last)
                    if u == 8 and not last:
                        x2t_low(c + 1, 1 - parity)
                    if u == 10 and not first:
                        result_of(c - 1)
                weigh_hidden(c, UNITS - 1)

            layer_norm(NCH, 0)
            dve.wait_ge(const_ready, 10)
            dve.wait_ge(small_in, 16 * 5)
            x2t_low(0, 0)
            for level in route_levels:
                level(0)
            in_chunk_pairs(dve, experts_of)
            result_of(NCH - 1)

        @block.tensor
        def _(pe):
            def split_product(ps, w, x, start=True, stop=True):
                (wh, wl), (xh, xl) = w, x
                nc.tensor.matmul(ps, wh, xh, start=start, stop=False)
                nc.tensor.matmul(ps, wl, xh, start=False, stop=False)
                return nc.tensor.matmul(ps, wh, xl, start=False, stop=stop)

            def transpose_norm(n, ps):
                pe.wait_ge(xn_ready, CB * n + CB)
                for i in range(CB):
                    ins = nc.tensor.transpose(ps[:, i * P:(i + 1) * P], xn[:, i, :], ident[:])
                ins.then_inc(xt_done, 1)

            def g_project(ring, chunk, bank_free):
                pe.wait_ge(xlo_ready, chunk + 1)
                for j in range(4):
                    s, value = bank_free[j // 2]
                    wait(pe, s, value + j % 2)
                    for i in range(2):
                        p = 2 * j + i
                        cols = slice(ring * 2 * P, (ring + 1) * 2 * P)
                        ins = split_product(bank[j][:, i * 2 * P:(i + 1) * 2 * P],
                                            (a_hi[:, p, :], a_lo[:, p, :]), (xnt_hi[:, cols], xnt_lo[:, cols]))
                    ins.then_inc(g_done, 1)

            def max_scores(t, b, half, k):
                pe.wait_ge(ghi_ready, 4 * half + k + 1)
                if b % 2 == 0 and k < 2:
                    pe.wait_ge(glo_ready, 4 * half + k + 1)
                wait(pe, max_ready, 4 * t + k - 1)
                pe.wait_ge(diag_ready, 2 * t + 2)
                for i in range(2):
                    ins = nc.tensor.matmul(scores_ps[k % 2][:, i * 2 * P:(i + 1) * 2 * P],
                                           g_hi[:, (b // 2) % 2, 2 * k + i, (b % 2) * P:(b % 2 + 1) * P],
                                           flat(diag_hi[:, b % CB, :, :], 3), start=True, stop=True)
                ins.then_inc(smax_done, 1)

            def transpose_max(t, parity):
                pe.wait_ge(max_ready, 4 * t + 4)
                wait(pe, x2_ready, t - 2)
                wait(pe, maxt_ready, t)
                nc.tensor.transpose(small_ps[0:HEADS, 0:P], row_max[:, parity, :], ident[:]).then_inc(maxt_done, 1)

            def scores(t, b, half, k, loads, projections):
                pairs, q = group(k)
                ps = st_ps[k % 2][:]
                if k == 0:
                    pe.wait_ge(maxrow_in[b % 2], 16 * loads)
                    pe.wait_ge(glo_ready, 4 * half + 4)
                wait(pe, exp_ready, 4 * t + k - 1)
                if projections is not None and k < 2:
                    pe.wait_ge(glo_ready, 4 * projections + k - 1)
                cols = slice((b % 2) * P, (b % 2 + 1) * P)
                split_product(ps, (diag_hi[:, b, q, :], diag_lo[:, b, q, :]),
                              (g_hi[:, b // 2, pairs, cols], g_lo[:, b // 2, pairs, cols]), stop=False)
                heads = max_row[0:1, b % 2, :, :].rearrange("a (h q) n -> a h q n", q=2)
                nc.tensor.matmul(ps, neg_ones[:], heads[:, pairs, q, :], start=False, stop=True).then_inc(st_done, 1)

            def weigh(t, b, k, loads):
                pe.wait_ge(exp_ready, 4 * t + k + 1)
                wait(pe, norm_ready, 4 * t + k - 1)
                if k == 0:
                    pe.wait_ge(keys_in[b], 16 * loads)
                for i in range(4):
                    ins = nc.tensor.matmul(u_ps[k % 2][:, i * (CD + 1):(i + 1) * (CD + 1)], probs_t[:, k, i, :],
                                           ctx_keys[:, b, :], start=True, stop=True)
                ins.then_inc(u_done, 1)

            def transpose_u(t, parity, r):
                pe.wait_ge(norm_ready, 4 * t + 2 * r + 2)
                wait(pe, ut_ready, 2 * t + r)
                for i in range(4):
                    ins = nc.tensor.transpose(ut_ps[:, i * P:(i + 1) * P],
                                              u_norm[:, parity, 4 * r + i, :, :].rearrange("p q d -> p (q d)"), ident[:])
                ins.then_inc(ut_done, 1)

            def project_out(t, parity, maxima):
                pe.wait_ge(ut_ready, 2 * t + 2)
                pe.wait_ge(maxt_ready, maxima)
                ps = small_ps[:, D:2 * D]
                nc.tensor.matmul(ps, ones_row[:], bo_gated[:], start=True, stop=False)
                for p in range(PAIRS):
                    ins = nc.tensor.matmul(ps, u_t[:, parity, p, :], c_pair[:, p, :], start=False, stop=p == PAIRS - 1)
                ins.then_inc(attn_done, 1)

            pe.wait_ge(weights_in, 16 * 6)
            for i in range(4):
                left, right = ((wq_pair, wk_diag), (wv_diag, wo_pair))[i // 2]
                for j in range(4):
                    p = 4 * (i % 2) + j
                    ins = nc.tensor.matmul(bank[i][:, j * P:(j + 1) * P], left[:, p, :], right[:, p, :],
                                           start=True, stop=True)
                ins.then_inc(fold_done, 1)
            pe.wait_ge(const_ready, 7)
            transpose_norm(0, ut_ps)
            pe.wait_ge(alo_ready, 2)
            pe.wait_ge(c_ready, 2)
            pe.wait_ge(bo_ready, 1)
            g_project(0, 0, ((glo_ready, -2), (glo_ready, -2)))
            g_project(1, 0, ((glo_ready, 1), (glo_ready, 3)))
            for b in range(2):
                for k in range(4):
                    if b == 0 and k < 2:
                        pe.wait_ge(glo_ready, 8)
                    max_scores(b, b, 0, k)
            transpose_max(0, 0)

            def attention(c, first, last):
                for b in range(CB):
                    t = CB * c + b
                    for k in range(4):
                        if k == 2 and not (last and b == CB - 1):
                            transpose_max(t + 1, (b + 1) % 2)
                        if b == 1 and k == 3 and not last:
                            pe.wait_ge(ut_ready, 2 * t)
                            transpose_norm(c + 1, ut_ps)
                        if not (last and b >= 2):
                            max_scores(t + 2, b + 2, 2 * c + (b + 2) // 2, k)
                        if k == 0 and not (first and b == 0):
                            weigh(t - 1, (b - 1) % CB, 3, c + 1)
                        projections = {0: 2 * c + 2, 2: None if last else 2 * c + 3}.get(b)
                        scores(t, b, 2 * c + b // 2, k, 2 * c + b // 2 + 1, projections)
                        if k > 0:
                            weigh(t, b, k - 1, c + 1)
                        if k == 2 and not (first and b == 0):
                            transpose_u(t - 1, (b - 1) % 2, 1)
                        if k == 3:
                            if b == 1 and not last:
                                pe.wait_ge(xlo_ready, c + 2)
                            transpose_u(t, b % 2, 0)
                            if not (first and b == 0):
                                project_out(t - 1, (b - 1) % 2, t + 1 if last and b == CB - 1 else t + 2)
                    if b % 2 == 1 and not last:
                        g_project(b // 2, c + 1, ((max_ready, 4 * (t + 2) + 3), (exp_ready, 4 * t + 3)))

            in_chunks(pe, attention)
            weigh(NB - 1, CB - 1, 3, NCH)
            transpose_u(NB - 1, (NB - 1) % 2, 1)
            pe.wait_ge(x2_ready, NB - 1)
            project_out(NB - 1, (NB - 1) % 2, NB)

            def weight_halves(kind, u):
                cols = slice(kind * FW + u * P, kind * FW + (u + 1) * P)
                return w_hi[:, cols], w_lo[:, cols]

            x2_halves = [(x2t_hi[:, i, :], x2t_lo[:, i, :]) for i in range(2)]

            def route(c):
                pe.wait_ge(x2t_ready, c + 1)
                for i in range(CB):
                    ins = nc.tensor.matmul(misc_ps[:, i * NE:(i + 1) * NE], x2t[:, i * P:(i + 1) * P], router_w[:],
                                           start=True, stop=True)
                ins.then_inc(logits_done, 1)

            def transpose_weights(c):
                pe.wait_ge(parts_ready, c + 1)
                pe.wait_ge(logits_ready, c + 1)
                if not isinstance(c, int) or c > 1:
                    pe.wait_ge(result_ready, c - 1)
                ps = misc_ps[:].bitcast(BF16)
                for i in range(CB):
                    ins = nc.tensor.transpose(ps[0:3 * NE, i * P:(i + 1) * P],
                                              w_parts[:, i, :, :].rearrange("p a e -> p (a e)"), ident_bf[:])
                ins.then_inc(wt_done, 1)

            def down(c, u):
                n = UNITS * c + u
                pe.wait_ge(hidlo_ready, n + 1)
                if u == 0:
                    wait(pe, yt_ready, c)
                split_product(y_ps[:], weight_halves(2, u), (hid_hi[:, u % SLOTS, :], hid_lo[:, u % SLOTS, :]),
                              start=u == 0, stop=u == UNITS - 1).then_inc(down_done, 1)

            def transpose_y(c):
                pe.wait_ge(yt_ready, c + 1)
                for i in range(CB):
                    ins = nc.tensor.transpose(misc_ps[:, i * P:(i + 1) * P], y_t[:, i * P:(i + 1) * P], ident[:])
                ins.then_inc(y_done, 1)

            def experts_of(c, parity, first, last):
                for u in range(UNITS):
                    n = UNITS * c + u
                    if u == 0:
                        pe.wait_ge(x2lo_ready, c + 1)
                    wait(pe, silu_ready, free_of(2, c, u))
                    split_product(gate_ps[u % 2][:], weight_halves(0, u), x2_halves[parity]).then_inc(gate_done, 1)
                    wait(pe, gated_ready, free_of(2, c, u))
                    split_product(up_ps[u % 2][:], weight_halves(1, u), x2_halves[parity]).then_inc(up_done, 1)
                    if u > 0:
                        if u == 1:
                            pe.wait_ge(wt_ready, c + 1)
                        wait(pe, hid_ready, free_of(2, c, u))
                        nc.tensor.matmul(wbc_ps[u % 2][:], expand[:, u - 1, :], w_parts_t[:, parity, :],
                                         start=True, stop=True).then_inc(wbc_done, 1)
                    if u >= LAG:
                        down(c, u - LAG)
                    elif not first:
                        down(c - 1, UNITS - LAG + u)
                    if u == 0:
                        transpose_weights(c)
                    if u == 5 and not last:
                        pe.wait_ge(wt_ready, c + 1)
                        transpose_norm(NCH + c + 1, misc_ps)
                    if u == 7 and not last:
                        route(c + 1)
                    if u == 9 and not first:
                        if last:
                            pe.wait_ge(wt_ready, c + 1)
                        else:
                            pe.wait_ge(logits_ready, c + 2)
                        transpose_y(c - 1)

            pe.wait_ge(x2_ready, NB)
            pe.wait_ge(wsplit_ready, NB)
            pe.wait_ge(const_ready, 10)
            transpose_norm(NCH, misc_ps)
            route(0)
            in_chunk_pairs(pe, experts_of)
            for u in range(UNITS - LAG, UNITS):
                down(NCH - 1, u)
            transpose_y(NCH - 1)


def kernel(x, ctx_512, g_xattn, g_ffn, L0_xattn_Wq, L0_xattn_Wk, L0_xattn_Wv, L0_xattn_Wo, L0_xattn_bo,
           L0_ffn_gate_w, L0_ffn_gate_bias, L0_ffn_expert_gate, L0_ffn_expert_up, L0_ffn_expert_down,
           L0_ffn_shared_gate, L0_ffn_shared_up, L0_ffn_shared_down):
    import numpy as np
    import concourse.bacc as bacc
    from concourse.bass_utils import run_bass_kernel_spmd

    lay = np.ascontiguousarray
    ctx = np.asarray(ctx_512)

    def up(w, shared):
        return np.concatenate([np.asarray(shared).T, np.asarray(w).reshape(NE * EI, D).T], axis=1)

    down = np.concatenate([np.asarray(L0_ffn_shared_down).T,
                           np.asarray(L0_ffn_expert_down).transpose(0, 2, 1).reshape(NE * EI, D)], axis=0)
    down = down.reshape(UNITS, P, D).transpose(1, 0, 2).reshape(P, FW)
    experts = np.concatenate([up(L0_ffn_expert_gate, L0_ffn_shared_gate), up(L0_ffn_expert_up, L0_ffn_shared_up), down],
                             axis=1)
    arrays = {
        "x": lay(x), "ctx_nat": lay(ctx.transpose(1, 0, 2)), "ctx_t": lay(ctx.reshape(NB * P, CD).T),
        "g_xattn": lay(g_xattn), "g_ffn": lay(g_ffn), "wq_t": lay(np.asarray(L0_xattn_Wq).T),
        "wk_t": lay(np.asarray(L0_xattn_Wk).T), "wv_t": lay(np.asarray(L0_xattn_Wv).T), "wo": lay(L0_xattn_Wo),
        "bo": lay(L0_xattn_bo), "router_t": lay(np.asarray(L0_ffn_gate_w).T), "router_bias": lay(L0_ffn_gate_bias),
        "experts": lay(experts),
    }
    nc = bacc.Bacc("TRN2", target_bir_lowering=False, num_devices=1)
    ins = [nc.dram_tensor(n, a.shape, F32, kind="ExternalInput").ap() for n, a in arrays.items()]
    out = nc.dram_tensor("out", (NB, P, D), F32, kind="ExternalOutput").ap()
    build(nc, *ins, out)
    r = run_bass_kernel_spmd(nc, [arrays], core_ids=[0])
    return r.results[0]["out"]
```

```python
from contextlib import ExitStack

import concourse.bass as bass
from concourse import mybir

F32 = mybir.dt.float32
F32R = mybir.dt.float32r
BF16 = mybir.dt.bfloat16
I32 = mybir.dt.int32
ACT = mybir.ActivationFunctionType
ALU = mybir.AluOpType
AX_X = mybir.AxisListType.X

P = 128
NB = 32
D = 128
HEADS, HD, CD = 16, 64, 64
PAIRS = HEADS // 2
CB = 4
NCH = NB // CB
CT = CB * P
NE, EI = 32, 64
GROUPS, GE = 4, 8
GROUPS_TAKEN = 2
UNITS = NE // 2 + 1
FW = UNITS * P
WCOLS = 3 * FW
WSTEP = WCOLS // NB
SCALE = float(HD) ** -0.5
ROUTED_SCALING = 2.5
EPS = 1e-5
LOWEST, PICKED = -1.0e30, 3.0e38
GUESS_SCALE = 1.36 * 2.0 ** -66

NEWTON_STEPS = 3
LN_STEPS = 2 * CB + 5 + 3 * NEWTON_STEPS
ROUTE_STEPS = 53
WARM_UP, GAP_1, GAP_2 = 5, 2, 1
LAG = 4
SLOTS = 6
ROUTE_FROM = 7
HIDS = 3
LN_LEVELS = 5 + 3 * NEWTON_STEPS
LN_SPREAD = 5
ROUTE_SPREAD, ROUTE_LEVELS = 5, 6
LN2_SPREAD = 8


def build(nc, x, ctx_nat, ctx_t, g_xattn, g_ffn, wq_t, wk_t, wv_t, wo, bo, router_t, router_bias, experts, out):
    with ExitStack() as stack:
        def sb(name, shape, dt=F32):
            return stack.enter_context(nc.sbuf_tensor(name, shape, dt))

        def sem(name):
            return stack.enter_context(nc.semaphore(name))

        def raw(ap):
            return ap.bitcast(F32)

        def flat(ap, n):
            return ap.rearrange({3: "p a b -> p (a b)", 4: "p a b c -> p (a b c)"}[n])

        x_sb = sb("x_sb", [P, NB, D])
        ident = sb("ident", [P, P])
        ident_bf = sb("ident_bf", [P, P], BF16)
        neg_ones = sb("neg_ones", [1, P], F32R)
        ones_col = sb("ones_col", [P, 1])
        gates = sb("gates", [P, 2])
        tanh_g = sb("tanh_g", [P, 2])
        bo_bc = sb("bo_bc", [P, D])
        bo_gated = sb("bo_gated", [P, D])
        area = sb("area", [P, 6, 1024])
        wq_pair, wk_diag, wv_diag, wo_pair = (
            area[:, i, :].rearrange("p (h n) -> p h n", h=PAIRS) for i in range(4))
        probs_t = area[:, 0:2, :].rearrange("p a n -> p (a n)").rearrange("p (k h n) -> p k h n", k=4, h=4)
        u_norm = area[:, 2:4, :].rearrange("p a (h q d) -> p a h q d", h=PAIRS, q=2)
        u_t = area[:, 4:6, :].rearrange("p a (h n) -> p a h n", h=PAIRS)
        tokens = area.rearrange("p a n -> p (a n)").rearrange("p (a n) -> p a n", n=CT)
        silu_g, gated, hid = tokens[:, 0:2, :], tokens[:, 2:2 + HIDS, :], tokens[:, 2 + HIDS:2 + 2 * HIDS, :]
        result, y_t = tokens[:, 2 + 2 * HIDS, :], tokens[:, 3 + 2 * HIDS, :]
        a_hi = sb("a_hi", [P, PAIRS, P], F32R)
        a_lo = sb("a_lo", [P, PAIRS, P], F32R)
        c_pair = sb("c_pair", [P, PAIRS, D])
        ctx_keys = sb("ctx_keys", [P, CB, CD + 1])
        ctx_raw = sb("ctx_raw", [P, CB, P])
        diag_hi = sb("diag_hi", [P, CB, 2, P], F32R)
        diag_lo = sb("diag_lo", [P, CB, 2, P], F32R)
        bn6 = sb("bn6", [P, 2, CB, 6])
        mean_var = sb("mean_var", [P, 2, CB, 2])
        var_eps = sb("var_eps", [P, 2, CB])
        half_var = sb("half_var", [P, 2, CB])
        rsqrt_bits = sb("rsqrt_bits", [P, 2, CB])
        guess = sb("guess", [P, 2, NEWTON_STEPS, CB])
        newton = sb("newton", [P, 2, 2, CB])
        mean1 = sb("mean1", [P, CB])
        rstd = sb("rstd", [P, CB])
        mean2 = sb("mean2", [P, NB])
        rstd2 = sb("rstd2", [P, NB])
        xn = sb("xn", [P, CB, D])
        xnt_hi = sb("xnt_hi", [P, CT], F32R)
        xnt_lo = sb("xnt_lo", [P, CT], F32R)
        halves = sb("halves", [P, 2, 2 * PAIRS * 2 * P], F32R)
        g_hi, g_lo = (halves[:, i, :].rearrange("p (r h n) -> p r h n", r=2, h=PAIRS) for i in range(2))
        hid_hi, hid_lo = (halves[:, i, 0:SLOTS * CT].rearrange("p (s n) -> p s n", s=SLOTS) for i in range(2))
        row_max = sb("row_max", [P, 2, HEADS])
        max_t = sb("max_t", [HEADS, 2, P], F32R)
        max_row = sb("max_row", [1, 2, HEADS, P], F32R)
        inv_sum = sb("inv_sum", [P, 4, 4])
        w_raw = sb("w_raw", [P, 2, WSTEP])
        w_hi = sb("w_hi", [P, WCOLS], F32R)
        w_lo = sb("w_lo", [P, WCOLS], F32R)
        router_w = sb("router_w", [P, NE])
        bias_bc = sb("bias_bc", [P, NE])
        expand = sb("expand", [3 * NE, NE // 2, P], BF16)
        x2t = sb("x2t", [P, CT])
        x2t_hi = sb("x2t_hi", [P, 2, CT], F32R)
        x2t_lo = sb("x2t_lo", [P, 2, CT], F32R)
        logits = sb("logits", [P, CB * NE])
        logits_low = sb("logits_low", [P, CB * NE])
        tanh_half = sb("tanh_half", [P, CB * NE])
        silu_low = sb("silu_low", [P, CB * NE])
        sig = sb("sig", [P, 5, CB * NE])
        score = sb("score", [P, CB, NE])
        choice = sb("choice", [P, CB, NE])
        top_in_group = sb("top_in_group", [P, CB, GROUPS, 8])
        group_score = sb("group_score", [P, CB, GROUPS + 6])
        group_top = sb("group_top", [P, CB, 8])
        group_pick = sb("group_pick", [P, CB, 8])
        group_left = sb("group_left", [P, CB, GROUPS + 6])
        group_mask = sb("group_mask", [P, CB, GROUPS])
        masked = sb("masked", [P, CB, NE])
        expert_top = sb("expert_top", [P, CB, 8])
        expert_left = sb("expert_left", [P, CB, NE])
        weight = sb("weight", [P, 2, CB, NE])
        weight_sum = sb("weight_sum", [P, 2, CB])
        weight_inv = sb("weight_inv", [P, CB])
        rest = sb("rest", [P, 2, CB, NE])
        w_parts = sb("w_parts", [P, CB, 3, NE], BF16)
        w_parts_t = sb("w_parts_t", [3 * NE, 2, CT], BF16)

        bank = [stack.enter_context(nc.psum_tensor(f"bank{i}", [P, 512], F32)) for i in range(8)]
        scores_ps, st_ps, u_ps, ut_ps, small_ps = bank[0:2], bank[2:4], bank[4:6], bank[6], bank[7]
        gate_ps, up_ps, wbc_ps, y_ps, misc_ps = bank[0:2], bank[2:4], bank[4:6], bank[6], bank[7]

        x_in = [sem("x_in0"), sem("x_in1")]
        wqk_in, wvo_in, small_in = sem("wqk_in"), sem("wvo_in"), sem("small_in")
        keys_in = [sem(f"keys_in{b}") for b in range(CB)]
        raw_in = [sem(f"raw_in{b}") for b in range(CB)]
        wraw_in = [sem("wraw_in0"), sem("wraw_in1")]
        maxrow_in = [sem("maxrow_in0"), sem("maxrow_in1")]
        result_free = sem("result_free")
        zeroed, const_step, const_ready = sem("zeroed"), sem("const_step"), sem("const_ready")
        tanh_ready, bo_ready = sem("tanh_ready"), sem("bo_ready")
        fold_done, ahi_ready, alo_ready, c_ready = (
            sem("fold_done"), sem("ahi_ready"), sem("alo_ready"), sem("c_ready"))
        ln_step, xn_ready = [sem("ln_step"), sem("ln2_step")], sem("xn_ready")
        xt_done, xhi_ready, xlo_ready = sem("xt_done"), sem("xhi_ready"), sem("xlo_ready")
        g_done, ghi_ready, glo_ready = sem("g_done"), sem("ghi_ready"), sem("glo_ready")
        diaghi_ready, diag_ready = sem("diaghi_ready"), sem("diag_ready")
        warm_ready = sem("warm_ready")
        waits_passed, loads_begun = sem("waits_passed"), sem("loads_begun")
        wsplit_hi, wsplit_ready = sem("wsplit_hi"), sem("wsplit_ready")
        smax_done, max_ready = sem("smax_done"), sem("max_ready")
        maxt_done, maxt_ready = sem("maxt_done"), sem("maxt_ready")
        st_done, exp_ready = sem("st_done"), sem("exp_ready")
        u_done, inv_ready, norm_ready = sem("u_done"), sem("inv_ready"), sem("norm_ready")
        ut_done, ut_ready = sem("ut_done"), sem("ut_ready")
        bias_added, attn_done, x2_ready = sem("bias_added"), sem("attn_done"), sem("x2_ready")
        x2t_ready, x2hi_ready, x2lo_ready = sem("x2t_ready"), sem("x2hi_ready"), sem("x2lo_ready")
        logits_done, logits_ready, sig_ready = sem("logits_done"), sem("logits_ready"), sem("sig_ready")
        route_step, parts_ready = sem("route_step"), sem("parts_ready")
        wt_done, wt_ready = sem("wt_done"), sem("wt_ready")
        gate_done, up_done, wbc_done = sem("gate_done"), sem("up_done"), sem("wbc_done")
        silu_ready, gated_ready = sem("silu_ready"), sem("gated_ready")
        hid_ready, hidhi_ready, hidlo_ready = sem("hid_ready"), sem("hidhi_ready"), sem("hidlo_ready")
        down_done, yt_ready = sem("down_done"), sem("yt_ready")
        y_done, result_ready = sem("y_done"), sem("result_ready")

        def wait(eng, s, value):
            if isinstance(value, int) and value <= 0:
                return
            eng.wait_ge(s, value)

        x_dram = x.rearrange("b n d -> n b d")
        out_dram = out.rearrange("b n d -> n b d")

        def group(k):
            return slice(4 * (k // 2), 4 * (k // 2) + 4), k % 2

        def in_chunks(eng, body):
            body(0, True, False)
            with eng.Fori(1, NCH - 1) as c:
                body(c, False, False)
            body(NCH - 1, False, True)

        def in_chunk_pairs(eng, body):
            body(0, 0, True, False)
            with eng.Fori(0, NCH // 2 - 1) as i:
                body(2 * i + 1, 1, False, False)
                body(2 * i + 2, 0, False, False)
            body(NCH - 1, (NCH - 1) % 2, False, True)

        def free_of(slots, c, u):
            if u >= slots:
                return UNITS * c + u - slots + 1
            before = max(v for v in range(UNITS) if v % slots == u)
            return UNITS * c - UNITS + before + 1

        block = stack.enter_context(nc.Block())

        @block.sync
        def _(sp):
            def wait_first(s, value):
                wait(sp, s, value)
                sp.sem_inc(loads_begun, 1)

            def load_keys(b, t):
                sp.dma_start(ctx_keys[:, b, 0:CD], ctx_nat[:, bass.ds(t, 1), :].rearrange("m a d -> m (a d)"))\
                    .then_inc(keys_in[b], 16)

            def load_raw(b, tokens):
                for q in range(2):
                    sp.dma_start(ctx_raw[q * CD:q * CD + CD, b, :], ctx_t[:, bass.ds(tokens, P)])\
                        .then_inc(raw_in[b], 16)

            def load_weights(slot, cols):
                sp.dma_start(w_raw[:, slot, :], experts[:, bass.ds(cols, WSTEP)]).then_inc(wraw_in[slot], 16)

            def load_max_row(t, parity, before):
                wait_first(maxt_ready, t + 1)
                wait_first(st_done, 4 * before + 4)
                sp.dma_start(raw(max_row[0:1, parity, :, :]), raw(max_t[:, parity, :])).then_inc(maxrow_in[parity], 16)

            def load_diag(diag, w, q, arrived):
                rows = slice(q * HD, q * HD + HD)
                sp.dma_start(diag[rows, :, q * CD:q * CD + CD],
                             w.rearrange("(p q r) n -> q r p n", q=2, r=HD)[q]).then_inc(arrived, 16)

            sp.dma_start(wq_pair, wq_t.rearrange("(p r) n -> r p n", r=P)).then_inc(wqk_in, 16)
            sp.dma_start(x_sb[:, 0:CB, :], x_dram[:, 0:CB, :]).then_inc(x_in[0], 16)
            sp.wait_ge(zeroed, 2)
            for q in range(2):
                load_diag(wk_diag, wk_t, q, wqk_in)
            for n, g in enumerate((g_xattn, g_ffn)):
                sp.dma_start(gates[:, n:n + 1], g.rearrange("(a n) -> a n", a=1).broadcast_to([P, 1]))\
                    .then_inc(small_in, 16)
            sp.dma_start(bo_bc[:], bo.rearrange("(a n) -> a n", a=1).broadcast_to([P, D])).then_inc(small_in, 16)
            sp.dma_start(bias_bc[:], router_bias.rearrange("(a n) -> a n", a=1).broadcast_to([P, NE]))\
                .then_inc(small_in, 16)
            sp.dma_start(router_w[:], router_t).then_inc(small_in, 16)
            for b in range(2):
                load_raw(b, b * P)
            for q in range(2):
                load_diag(wv_diag, wv_t, q, wvo_in)
            sp.dma_start(wo_pair, wo.rearrange("(p r) n -> r p n", r=P)).then_inc(wvo_in, 16)
            for b in range(2, CB):
                load_raw(b, b * P)
            for b in range(CB - 1):
                load_keys(b, b)
            sp.dma_start(x_sb[:, CB:NB, :], x_dram[:, CB:NB, :]).then_inc(x_in[1], 16)
            for slot in range(2):
                load_weights(slot, slot * WSTEP)
            load_max_row(0, 0, -2)

            def attention(c, first, last):
                for b in range(CB):
                    t = CB * c + b
                    if not last:
                        wait_first(diag_ready, 2 * t + 2)
                        load_raw(b, (t + CB) * P)
                    if not (last and b >= 2):
                        wait_first(wsplit_ready, t + 1)
                        load_weights(b % 2, (t + 2) * WSTEP)
                    if not (last and b == CB - 1):
                        load_max_row(t + 1, (b + 1) % 2, t - 1)
                    if not (last and b > 0):
                        wait_first(u_done, 4 * t)
                        load_keys((b - 1) % CB, t - 1 + CB)

            in_chunks(sp, attention)

            sp.sem_inc(result_free, 16)
            with sp.Fori(0, NCH) as c:
                wait_first(result_ready, c + 1)
                sp.dma_start(out_dram[:, bass.ds(c * CB, CB), :], result.rearrange("p (b d) -> p b d", b=CB))\
                    .then_inc(result_free, 16)
            sp.wait_ge(result_free, 16 * NCH + 16)

        @block.gpsimd
        def _(pool):
            nc.gpsimd.memset(wk_diag, 0.0).then_inc(zeroed, 1)
            nc.gpsimd.memset(wv_diag, 0.0).then_inc(zeroed, 1)
            nc.gpsimd.memset(ones_col[:], 1.0).then_inc(const_step, 1)
            nc.gpsimd.memset(ident[:], 0.0).then_inc(const_step, 1)
            nc.gpsimd.memset(ident_bf[:], 0.0).then_inc(const_step, 1)
            nc.gpsimd.memset(expand[:], 0.0).then_inc(const_step, 1)
            nc.gpsimd.memset(raw(neg_ones[:]), -1.0).then_inc(const_ready, 1)
            nc.gpsimd.memset(ctx_keys[:, :, CD:CD + 1], 1.0).then_inc(const_ready, 1)
            nc.gpsimd.memset(group_score[:], LOWEST).then_inc(const_ready, 1)
            nc.gpsimd.memset(group_pick[:], LOWEST).then_inc(const_ready, 1)
            pool.wait_ge(const_step, 4)
            for m in (ident, ident_bf):
                nc.gpsimd.affine_select(out=m[:], in_=m[:], compare_op=ALU.not_equal, fill=1.0, base=0,
                                        pattern=[[-1, P]], channel_multiplier=1).then_inc(const_ready, 1)
            nc.gpsimd.memset(raw(diag_hi[:]), 0.0).then_inc(zeroed, 1)
            nc.gpsimd.memset(raw(diag_lo[:]), 0.0).then_inc(zeroed, 1)

            def split_context(b, t, c):
                pool.wait_ge(raw_in[b], 32 * c + 32)
                wait(pool, bias_added, t - CB + 1)
                wait(pool, st_done, 4 * (t - CB) + 4)
                for q in range(2):
                    rows = slice(q * CD, q * CD + CD)
                    nc.gpsimd.tensor_tensor(diag_hi[rows, b, q, :], ctx_raw[rows, b, :],
                                            ones_col[rows, :].broadcast_to([CD, P]), ALU.mult)\
                        .then_inc(diaghi_ready, 1)
                pool.wait_ge(diaghi_ready, 2 * t + 2)
                for q in range(2):
                    rows = slice(q * CD, q * CD + CD)
                    nc.gpsimd.tensor_tensor(diag_lo[rows, b, q, :], ctx_raw[rows, b, :],
                                            raw(diag_hi[rows, b, q, :]), ALU.subtract).then_inc(diag_ready, 1)

            def split_weights(slot, t, nth, contexts):
                cols = bass.ds(t * WSTEP, WSTEP)
                pool.wait_ge(wraw_in[slot], 16 * nth + 16)
                pool.wait_ge(diag_ready, contexts)
                nc.gpsimd.tensor_tensor(w_hi[:, cols], w_raw[:, slot, :], ones_col[:].broadcast_to([P, WSTEP]),
                                        ALU.mult).then_inc(wsplit_hi, 1)
                pool.wait_ge(wsplit_hi, t + 1)
                nc.gpsimd.tensor_tensor(w_lo[:, cols], w_raw[:, slot, :], raw(w_hi[:, cols]), ALU.subtract)\
                    .then_inc(wsplit_ready, 1)

            def add_bias(t, c):
                pool.wait_ge(xn_ready, CB * (c + 1))
                tile = x_sb[:, bass.ds(t, 1), :].rearrange("p a d -> p (a d)")
                nc.gpsimd.tensor_tensor(tile, tile, bo_gated[:], ALU.add).then_inc(bias_added, 1)

            pool.wait_ge(zeroed, 4)
            for b in range(CB):
                split_context(b, b, 0)
            pool.wait_ge(diag_ready, 2 * CB)
            for part in range(3):
                rows = expand[part * NE:(part + 1) * NE].rearrange("j u (e i) -> j u e i", e=2)
                nc.gpsimd.affine_select(out=rows, in_=rows, compare_op=ALU.not_equal, fill=1.0, base=0,
                                        pattern=[[-2, NE // 2], [-1, 2], [0, EI]], channel_multiplier=1)\
                    .then_inc(const_ready, 1)
            pool.wait_ge(const_ready, 9)

            def attention(c, first, last):
                for b in range(CB):
                    t = CB * c + b
                    split_weights(b % 2, t, 2 * c + b // 2, 2 * NB if last else 2 * (t + CB))
                    add_bias(t, c)
                    if not last:
                        split_context(b, t + CB, c + 1)

            pool.wait_ge(bo_ready, 1)
            pool.wait_ge(x_in[1], 16)
            in_chunks(pool, attention)

            def experts_low(c):
                for u in range(UNITS):
                    n = UNITS * c + u
                    pool.wait_ge(hidhi_ready, n + 1)
                    wait(pool, down_done, free_of(SLOTS, c, u))
                    nc.gpsimd.tensor_tensor(hid_lo[:, u % SLOTS, :], hid[:, u % HIDS, :], raw(hid_hi[:, u % SLOTS, :]),
                                            ALU.subtract).then_inc(hidlo_ready, 1)

            experts_low(0)
            with pool.Fori(1, NCH) as c:
                experts_low(c)

        @block.scalar
        def _(act):
            def xt_high(i):
                act.wait_ge(xt_done, i + 1)
                wait(act, g_done, 8 * i)
                nc.scalar.activation(xnt_hi[:], ut_ps[:], ACT.Copy).then_inc(xhi_ready, 1)

            def g_high(g, ring):
                for j in range(4):
                    act.wait_ge(g_done, 4 * g + j + 1)
                    wait(act, st_done, 8 * g - 8)
                    nc.scalar.activation(g_hi[:, ring, 2 * j:2 * j + 2, :],
                                         bank[j][:].rearrange("p (h n) -> p h n", h=2), ACT.Copy)\
                        .then_inc(ghi_ready, 1)

            def max_out(t, parity, loads_before):
                act.wait_ge(maxt_done, t + 1)
                wait(act, maxrow_in[parity], 16 * loads_before)
                nc.scalar.activation(max_t[:, parity, :], small_ps[0:HEADS, 0:P], ACT.Copy).then_inc(maxt_ready, 1)

            def ut_out(t, parity, r):
                act.wait_ge(ut_done, 2 * t + r + 1)
                wait(act, attn_done, t - 1)
                nc.scalar.activation(u_t[:, parity, 4 * r:4 * r + 4, :],
                                     ut_ps[:].rearrange("p (h n) -> p h n", h=4), ACT.Copy).then_inc(ut_ready, 1)

            def x2t_out(c, ps=misc_ps):
                act.wait_ge(xt_done, NCH + c + 1)
                nc.scalar.activation(x2t[:], ps[:], ACT.Copy).then_inc(x2t_ready, 1)

            def x2t_high(c, parity):
                act.wait_ge(x2t_ready, c + 1)
                wait(act, up_done, UNITS * (c - 1))
                nc.scalar.activation(x2t_hi[:, parity, :], x2t[:], ACT.Copy).then_inc(x2hi_ready, 1)

            def logits_out(c, ps=misc_ps):
                act.wait_ge(logits_done, c + 1)
                nc.scalar.activation(logits[:], ps[:, 0:CB * NE], ACT.Copy).then_inc(logits_ready, 1)

            def sigmoids(c):
                act.wait_ge(logits_ready, c + 1)
                nc.scalar.activation(tanh_half[:], logits[:], ACT.Tanh, scale=0.5).then_inc(sig_ready, 1)
                act.wait_ge(route_step, ROUTE_STEPS * c + 1)
                nc.scalar.activation(silu_low[:], logits_low[:], ACT.Silu).then_inc(sig_ready, 1)

            act.wait_ge(small_in, 16 * 5)
            nc.scalar.activation(tanh_g[:], gates[:], ACT.Tanh).then_inc(tanh_ready, 1)
            act.wait_ge(tanh_ready, 1)
            nc.scalar.activation(bo_gated[:], bo_bc[:], ACT.Copy, scale=tanh_g[:, 0:1]).then_inc(bo_ready, 1)
            for i in range(2):
                act.wait_ge(fold_done, i + 1)
                half = slice(4 * i, 4 * i + 4)
                nc.scalar.activation(a_hi[:, half, :], scores_ps[i][:].rearrange("p (h n) -> p h n", h=4), ACT.Copy,
                                     scale=SCALE).then_inc(ahi_ready, 1)
            xt_high(0)
            g_high(0, 0)
            for i in range(2):
                act.wait_ge(fold_done, i + 3)
                nc.scalar.activation(c_pair[:, 4 * i:4 * i + 4, :], u_ps[i][:].rearrange("p (h n) -> p h n", h=4),
                                     ACT.Copy, scale=tanh_g[:, 0:1]).then_inc(c_ready, 1)
            max_out(0, 0, 0)
            g_high(1, 1)

            def attention(c, first, last):
                for b in range(CB):
                    t = CB * c + b
                    for k in range(4):
                        if k == 2 and not (last and b == CB - 1):
                            max_out(t + 1, (b + 1) % 2, 2 * c + (b - 1) // 2 + 1)
                        act.wait_ge(st_done, 4 * t + k + 1)
                        wait(act, u_done, 4 * t + k - 3)
                        nc.scalar.activation(probs_t[:, k, :, :],
                                             st_ps[k % 2][:].rearrange("p (h n) -> p h n", h=4), ACT.Exp)\
                            .then_inc(exp_ready, 1)
                        if b == 1 and k == 3:
                            if last:
                                x2t_out(0, ut_ps)
                            else:
                                xt_high(c + 1)
                        if last and b == 2:
                            if k == 0:
                                x2t_high(0, 0)
                            if k == 1:
                                logits_out(0, ut_ps)
                            if k == 2:
                                sigmoids(0)
                        if k == 2 and not (first and b == 0):
                            ut_out(t - 1, (b - 1) % 2, 1)
                        if k == 3:
                            ut_out(t, b % 2, 0)
                    if b % 2 == 1 and not last:
                        g_high(2 * c + 2 + b // 2, b // 2)

            in_chunks(act, attention)
            ut_out(NB - 1, (NB - 1) % 2, 1)

            def weights_out(c, parity):
                act.wait_ge(wt_done, c + 1)
                wait(act, wbc_done, (UNITS - 1) * (c - 1))
                nc.scalar.activation(w_parts_t[:, parity, :], misc_ps[:].bitcast(BF16)[0:3 * NE, 0:CT], ACT.Copy)\
                    .then_inc(wt_ready, 1)

            def hidden_high(c, u):
                act.wait_ge(hid_ready, UNITS * c + u + 1)
                wait(act, down_done, free_of(SLOTS, c, u))
                nc.scalar.activation(hid_hi[:, u % SLOTS, :], hid[:, u % HIDS, :], ACT.Copy).then_inc(hidhi_ready, 1)

            def y_out(c):
                act.wait_ge(down_done, UNITS * (c + 1))
                nc.scalar.activation(y_t, y_ps[:], ACT.Copy).then_inc(yt_ready, 1)

            def experts_of(c, parity, first, last):
                for u in range(UNITS):
                    act.wait_ge(gate_done, UNITS * c + u + 1)
                    wait(act, gated_ready, free_of(2, c, u))
                    nc.scalar.activation(silu_g[:, u % 2, :], gate_ps[u % 2][:], ACT.Silu).then_inc(silu_ready, 1)
                    if u >= 2:
                        hidden_high(c, u - 2)
                    elif not first:
                        hidden_high(c - 1, UNITS - 2 + u)
                    if u == 0:
                        weights_out(c, parity)
                    if u == LAG - 1 and not first:
                        y_out(c - 1)
                    if not last:
                        if u == 2:
                            x2t_out(c + 1)
                        if u == 3:
                            x2t_high(c + 1, 1 - parity)
                        if u == 4:
                            logits_out(c + 1)
                        if u == 6:
                            sigmoids(c + 1)

            in_chunk_pairs(act, experts_of)
            for u in (UNITS - 2, UNITS - 1):
                hidden_high(NCH - 1, u)
            y_out(NCH - 1)

        @block.vector
        def _(dve):
            def wait_first(s, value):
                dve.wait_ge(s, value)
                dve.sem_inc(waits_passed, 1)

            def ln_level(which, n, t, level):
                base, stepped = LN_STEPS * n, ln_step[which]
                v, w = var_eps[:, which, :], half_var[:, which, :]
                i, newton_op = divmod(level - 5, 3)
                if level == 0:
                    for b in range(CB):
                        nc.vector.bn_stats(bn6[:, which, b, :],
                                           x_sb[:, bass.ds(t + b, 1), :].rearrange("p a d -> p (a d)"))\
                            .then_inc(stepped, 1)
                elif level == 1:
                    wait_first(stepped, base + CB)
                    for b in range(CB):
                        nc.vector.bn_aggr(mean_var[:, which, b, :], bn6[:, which, b, :]).then_inc(stepped, 1)
                elif level == 2:
                    dve.wait_ge(stepped, base + 2 * CB)
                    nc.vector.tensor_scalar(v, mean_var[:, which, :, 1], EPS, None, ALU.add).then_inc(stepped, 1)
                    nc.vector.tensor_scalar(w, mean_var[:, which, :, 1], EPS, -0.5, ALU.add, ALU.mult)\
                        .then_inc(stepped, 1)
                elif level == 3:
                    dve.wait_ge(stepped, base + 2 * CB + 2)
                    nc.vector.tensor_scalar(rsqrt_bits[:, which, :].bitcast(I32), v.bitcast(I32), 1, 0x7fffffff,
                                            ALU.logical_shift_right, ALU.bitwise_xor).then_inc(stepped, 1)
                    nc.vector.tensor_copy(mean2[:, bass.ds(t, CB)] if which else mean1[:], mean_var[:, which, :, 0])\
                        .then_inc(stepped, 1)
                elif level == 4:
                    dve.wait_ge(stepped, base + 2 * CB + 4)
                    nc.vector.tensor_scalar(guess[:, which, 0, :], rsqrt_bits[:, which, :], GUESS_SCALE, None, ALU.mult)\
                        .then_inc(stepped, 1)
                else:
                    r, better = guess[:, which, i, :], guess[:, which, (i + 1) % NEWTON_STEPS, :]
                    if i == NEWTON_STEPS - 1:
                        better = rstd2[:, bass.ds(t, CB)] if which else rstd[:]
                    square, product = newton[:, which, 0, :], newton[:, which, 1, :]
                    dve.wait_ge(stepped, base + 2 * CB + 5 + 3 * i + newton_op)
                    if newton_op == 0:
                        ins = nc.vector.tensor_tensor(square, r, r, ALU.mult)
                    elif newton_op == 1:
                        ins = nc.vector.tensor_tensor(product, square, w, ALU.mult)
                    else:
                        ins = nc.vector.scalar_tensor_tensor(better, product, 1.5, r, ALU.add, ALU.mult)
                    ins.then_inc(stepped, 1)

            def ln_apply(n, t):
                dve.wait_ge(ln_step[0], LN_STEPS * (n + 1))
                wait(dve, xt_done, n)
                for b in range(CB):
                    nc.vector.tensor_scalar(xn[:, b, :], x_sb[:, bass.ds(t + b, 1), :].rearrange("p a d -> p (a d)"),
                                            mean1[:, b:b + 1], rstd[:, b:b + 1], ALU.subtract, ALU.mult)\
                        .then_inc(xn_ready, 1)

            def ln2_apply(n, t):
                dve.wait_ge(ln_step[1], LN_STEPS * (n + 1))
                wait(dve, xt_done, NCH + n)
                for b in range(CB):
                    nc.vector.tensor_scalar(xn[:, b, :], x_sb[:, bass.ds(t + b, 1), :].rearrange("p a d -> p (a d)"),
                                            mean2[:, bass.ds(t + b, 1)], rstd2[:, bass.ds(t + b, 1)],
                                            ALU.subtract, ALU.mult).then_inc(xn_ready, 1)

            def xt_low(i):
                dve.wait_ge(xhi_ready, i + 1)
                nc.vector.tensor_tensor(xnt_lo[:], ut_ps[:], raw(xnt_hi[:]), ALU.subtract).then_inc(xlo_ready, 1)

            def g_low(g, ring):
                for j in range(4):
                    dve.wait_ge(ghi_ready, 4 * g + j + 1)
                    nc.vector.tensor_tensor(g_lo[:, ring, 2 * j:2 * j + 2, :],
                                            bank[j][:].rearrange("p (h n) -> p h n", h=2),
                                            raw(g_hi[:, ring, 2 * j:2 * j + 2, :]), ALU.subtract)\
                        .then_inc(glo_ready, 1)

            def take_max(t, parity, k):
                dve.wait_ge(smax_done, 4 * t + k + 1)
                wait(dve, maxt_done, t - 1)
                nc.vector.tensor_reduce(row_max[:, parity, 4 * k:4 * k + 4],
                                        scores_ps[k % 2][:].rearrange("p (h m) -> p h m", h=4), AX_X, ALU.max)\
                    .then_inc(max_ready, 1)

            def normalise(t, parity, k):
                pairs, q = group(k)
                u = u_ps[k % 2][:, 0:4 * (CD + 1)].rearrange("p (h d) -> p h d", h=4)
                dve.wait_ge(u_done, 4 * t + k + 1)
                wait(dve, inv_ready, 4 * t + k - 3)
                nc.vector.reciprocal(inv_sum[:, k, :], u[:, :, CD]).then_inc(inv_ready, 1)
                dve.wait_ge(inv_ready, 4 * t + k + 1)
                wait(dve, ut_done, 2 * (t - 2) + k // 2 + 1)
                nc.vector.tensor_tensor(u_norm[:, parity, pairs, q, :], u[:, :, 0:CD],
                                        inv_sum[:, k, :].unsqueeze(2).broadcast_to([P, 4, CD]), ALU.mult)\
                    .then_inc(norm_ready, 1)

            def residual(t):
                dve.wait_ge(bias_added, t + 1)
                dve.wait_ge(attn_done, t + 1)
                tile = x_sb[:, bass.ds(t, 1), :].rearrange("p a d -> p (a d)")
                nc.vector.tensor_tensor(tile, small_ps[:, D:2 * D], tile, ALU.add).then_inc(x2_ready, 1)

            def step(ins):
                ins.then_inc(route_step, 1)
                counted[0] += 1

            def so_far(c, alone=False):
                (wait_first if alone else dve.wait_ge)(route_step, ROUTE_STEPS * c + counted[0])

            counted = [0]

            def logits_below(c):
                counted[0] = 0
                dve.wait_ge(logits_ready, c + 1)
                step(nc.vector.tensor_scalar(logits_low[:], logits[:], -1.0, None, ALU.min))

            low_inv, high, low, rise, risen = (sig[:, i, :] for i in range(5))

            def sigmoid_high(c):
                dve.wait_ge(sig_ready, 2 * c + 2)
                step(nc.vector.reciprocal(low_inv, logits_low[:]))
                step(nc.vector.tensor_scalar(high, tanh_half[:], 0.5, 0.5, ALU.mult, ALU.add))

            def sigmoid_low(c):
                so_far(c)
                step(nc.vector.tensor_tensor(low, silu_low[:], low_inv, ALU.mult))

            def sigmoid_rise(c):
                so_far(c)
                step(nc.vector.tensor_tensor(rise, high, low, ALU.subtract))

            def sigmoid_risen(c):
                so_far(c)
                step(nc.vector.scalar_tensor_tensor(risen, logits[:], -1.0, rise, ALU.is_gt, ALU.mult))

            def scores_of(c):
                so_far(c)
                step(nc.vector.tensor_tensor(flat(score[:], 3), low, risen, ALU.add))

            def choices(c):
                so_far(c)
                step(nc.vector.tensor_tensor(choice[:], score[:], bias_bc[:].unsqueeze(1).broadcast_to([P, CB, NE]),
                                             ALU.add))

            def best_in_groups(c):
                so_far(c, alone=True)
                for i in range(CB):
                    for g in range(GROUPS):
                        step(nc.vector.max(top_in_group[:, i, g, :], choice[:, i, g * GE:(g + 1) * GE]))

            def group_scores(c):
                so_far(c)
                step(nc.vector.tensor_tensor(group_score[:, :, 0:GROUPS], top_in_group[:, :, :, 0],
                                             top_in_group[:, :, :, 1], ALU.add))

            def best_groups(c):
                so_far(c, alone=True)
                for i in range(CB):
                    step(nc.vector.max(group_top[:, i, :], group_score[:, i, :]))

            def take_groups(c):
                so_far(c)
                step(nc.vector.tensor_copy(group_pick[:, :, 0:GROUPS_TAKEN], group_top[:, :, 0:GROUPS_TAKEN]))

            def mark_groups(c):
                so_far(c, alone=True)
                for i in range(CB):
                    step(nc.vector.match_replace(group_left[:, i, :], group_pick[:, i, :], group_score[:, i, :], PICKED))

            def mask_groups(c):
                so_far(c)
                step(nc.vector.tensor_scalar(group_mask[:], group_left[:, :, 0:GROUPS], PICKED, None, ALU.is_equal))

            def mask_experts(c):
                so_far(c)
                step(nc.vector.tensor_tensor(
                    flat(masked[:], 3).rearrange("p (b e) -> p b e", e=GE),
                    flat(choice[:], 3).rearrange("p (b e) -> p b e", e=GE),
                    flat(group_mask[:], 3).unsqueeze(2).broadcast_to([P, CB * GROUPS, GE]), ALU.mult))

            def best_experts(c):
                so_far(c, alone=True)
                for i in range(CB):
                    step(nc.vector.max(expert_top[:, i, :], masked[:, i, :]))

            def mark_experts(c):
                so_far(c, alone=True)
                for i in range(CB):
                    step(nc.vector.match_replace(expert_left[:, i, :], expert_top[:, i, :], masked[:, i, :], PICKED))

            def picked_scores(c):
                so_far(c)
                step(nc.vector.scalar_tensor_tensor(flat(weight[:, 0], 3), flat(expert_left[:], 3), PICKED,
                                                    flat(score[:], 3), ALU.is_equal, ALU.mult))

            def picked_sum(c):
                so_far(c)
                step(nc.vector.tensor_reduce(weight_sum[:, 0, :], weight[:, 0], AX_X, ALU.add))

            def picked_guard(c):
                so_far(c)
                step(nc.vector.tensor_scalar(weight_sum[:, 1, :], weight_sum[:, 0, :], 1e-20, None, ALU.add))

            def picked_inverse(c):
                so_far(c)
                step(nc.vector.reciprocal(weight_inv[:], weight_sum[:, 1, :]))

            def weights_of(c):
                so_far(c)
                step(nc.vector.scalar_tensor_tensor(weight[:, 1], weight[:, 0], ROUTED_SCALING,
                                                    weight_inv[:].unsqueeze(2).broadcast_to([P, CB, NE]),
                                                    ALU.mult, ALU.mult))

            def first_part(c):
                so_far(c)
                wait(dve, wt_done, c)
                step(nc.vector.tensor_copy(w_parts[:, :, 0, :], weight[:, 1]))

            def first_rest(c):
                so_far(c)
                step(nc.vector.tensor_tensor(rest[:, 0], weight[:, 1], w_parts[:, :, 0, :], ALU.subtract))

            def second_part(c):
                so_far(c)
                step(nc.vector.tensor_copy(w_parts[:, :, 1, :], rest[:, 0]))

            def second_rest(c):
                so_far(c)
                step(nc.vector.tensor_tensor(rest[:, 1], rest[:, 0], w_parts[:, :, 1, :], ALU.subtract))

            def third_part(c):
                so_far(c)
                nc.vector.tensor_copy(w_parts[:, :, 2, :], rest[:, 1]).then_inc(parts_ready, 1)
                assert counted[0] == ROUTE_STEPS

            route_levels = (
                logits_below, sigmoid_high, sigmoid_low, sigmoid_rise, sigmoid_risen, scores_of, choices,
                best_in_groups, group_scores, best_groups, take_groups, mark_groups, mask_groups, mask_experts,
                best_experts, mark_experts, picked_scores, picked_sum, picked_guard, picked_inverse, weights_of,
                first_part, first_rest, second_part, second_rest, third_part)

            def x2t_low(c, parity):
                dve.wait_ge(x2hi_ready, c + 1)
                nc.vector.tensor_tensor(x2t_lo[:, parity, :], x2t[:], raw(x2t_hi[:, parity, :]), ALU.subtract)\
                    .then_inc(x2lo_ready, 1)

            nc.vector.memset(c_pair[:, 0:4, :], 0.0).then_inc(warm_ready, 1)
            dve.wait_ge(x_in[0], 16)
            for level in range(LN_LEVELS):
                ln_level(0, 0, 0, level)
            ln_apply(0, 0)
            for i in range(2):
                dve.wait_ge(ahi_ready, i + 1)
                half = slice(4 * i, 4 * i + 4)
                nc.vector.scalar_tensor_tensor(a_lo[:, half, :], scores_ps[i][:].rearrange("p (h n) -> p h n", h=4), SCALE,
                                               raw(a_hi[:, half, :]), ALU.mult, ALU.subtract).then_inc(alo_ready, 1)
            xt_low(0)
            for b in range(2):
                g_low(b, b)
                for k in range(4):
                    take_max(b, b, k)
            dve.wait_ge(x_in[1], 16)
            dve.wait_ge(const_ready, 9)

            def attention(c, first, last):
                for b in range(CB):
                    t = CB * c + b
                    for k in range(4):
                        if not (last and b >= 2):
                            take_max(t + 2, b % 2, k)
                        if k > 0:
                            normalise(t, b % 2, k - 1)
                        elif not (first and b == 0):
                            normalise(t - 1, (b - 1) % 2, 3)
                        if k == 0 and not (first and b < 2):
                            residual(t - 2)
                        at = 4 * b + k
                        if at < LN_SPREAD and not last:
                            for level in range(at * LN_LEVELS // LN_SPREAD, (at + 1) * LN_LEVELS // LN_SPREAD):
                                ln_level(0, c + 1, t - b + CB, level)
                            if at == LN_SPREAD - 1:
                                ln_apply(c + 1, t - b + CB)
                        at -= 4 * CB - LN2_SPREAD
                        if at >= 0 and not first:
                            for level in range(at * LN_LEVELS // LN2_SPREAD, (at + 1) * LN_LEVELS // LN2_SPREAD):
                                ln_level(1, c - 1, t - b - CB, level)
                        if last:
                            if b == 0 and k == 3:
                                ln2_apply(0, 0)
                            if b == 2 and k == 1:
                                x2t_low(0, 0)
                            if b == 2 and k == 1:
                                route_levels[0](0)
                            at = 4 * b + k - (4 * CB - ROUTE_SPREAD)
                            if at >= 0:
                                for level in route_levels[1 + ROUTE_LEVELS * at:1 + ROUTE_LEVELS * (at + 1)]:
                                    level(0)
                        if b == 1 and k == 3 and not last:
                            xt_low(c + 1)
                    if b % 2 == 1 and not last:
                        g_low(2 * c + 2 + b // 2, b // 2)

            in_chunks(dve, attention)
            normalise(NB - 1, (NB - 1) % 2, 3)
            residual(NB - 2)
            residual(NB - 1)

            def levels_at(c, parity, u, place, first, last):
                if first and place == 1 and 1 <= u <= LN_LEVELS:
                    ln_level(1, NCH - 1, NB - CB, u - 1)
                if last:
                    return
                if u == 0 and place == 1:
                    ln2_apply(c + 1, CB * (c + 1))
                if u == 4 and place == 1:
                    x2t_low(c + 1, 1 - parity)
                if u == 5 and place == 1:
                    route_levels[0](c + 1)
                at, places, levels = 2 * (u - ROUTE_FROM) + place, 2 * (UNITS - ROUTE_FROM), len(route_levels) - 1
                if at >= 0:
                    for level in route_levels[1 + at * levels // places:1 + (at + 1) * levels // places]:
                        level(c + 1)

            def result_of(c):
                dve.wait_ge(y_done, c + 1)
                dve.wait_ge(result_free, 16 * c + 16)
                nc.vector.scalar_tensor_tensor(
                    result, misc_ps[:], tanh_g[:, 1:2],
                    x_sb[:, bass.ds(CB * c, CB), :].rearrange("p b d -> p (b d)"), ALU.mult, ALU.add)\
                    .then_inc(result_ready, 1)

            def gate_up(c, u):
                n = UNITS * c + u
                dve.wait_ge(silu_ready, n + 1)
                dve.wait_ge(up_done, n + 1)
                wait(dve, hid_ready, free_of(HIDS, c, u))
                nc.vector.tensor_tensor(gated[:, u % HIDS, :], silu_g[:, u % 2, :], up_ps[u % 2][:], ALU.mult)\
                    .then_inc(gated_ready, 1)

            def weigh_hidden(c, u):
                dve.wait_ge(gated_ready, UNITS * c + u + 1)
                wait(dve, hidlo_ready, free_of(HIDS, c, u))
                if u == 0:
                    nc.vector.tensor_copy(hid[:, u % HIDS, :], gated[:, u % HIDS, :]).then_inc(hid_ready, 1)
                else:
                    dve.wait_ge(wbc_done, (UNITS - 1) * c + u)
                    nc.vector.tensor_tensor(hid[:, u % HIDS, :], gated[:, u % HIDS, :], wbc_ps[u % 2][:], ALU.mult)\
                        .then_inc(hid_ready, 1)

            def experts_of(c, parity, first, last):
                for u in range(UNITS):
                    gate_up(c, u)
                    levels_at(c, parity, u, 0, first, last)
                    if u > 0:
                        weigh_hidden(c, u - 1)
                    elif not first:
                        weigh_hidden(c - 1, UNITS - 1)
                    levels_at(c, parity, u, 1, first, last)
                    if u == 6 and not first:
                        result_of(c - 1)

            in_chunk_pairs(dve, experts_of)
            weigh_hidden(NCH - 1, UNITS - 1)
            result_of(NCH - 1)

        @block.tensor
        def _(pe):
            def split_product(ps, w, x, start=True, stop=True):
                (wh, wl), (xh, xl) = w, x
                nc.tensor.matmul(ps, wh, xh, start=start, stop=False)
                nc.tensor.matmul(ps, wl, xh, start=False, stop=False)
                return nc.tensor.matmul(ps, wh, xl, start=False, stop=stop)

            def transpose_norm(n, ps):
                pe.wait_ge(xn_ready, CB * n + CB)
                for i in range(CB):
                    ins = nc.tensor.transpose(ps[:, i * P:(i + 1) * P], xn[:, i, :], ident[:])
                ins.then_inc(xt_done, 1)

            def g_project(ring, chunk, bank_free):
                pe.wait_ge(xlo_ready, chunk + 1)
                for j in range(4):
                    s, value = bank_free[j // 2]
                    wait(pe, s, value + j % 2)
                    if j % 2 == 0:
                        pe.wait_ge(alo_ready, j // 2 + 1)
                    for i in range(2):
                        p = 2 * j + i
                        cols = slice(ring * 2 * P, (ring + 1) * 2 * P)
                        ins = split_product(bank[j][:, i * 2 * P:(i + 1) * 2 * P],
                                            (a_hi[:, p, :], a_lo[:, p, :]), (xnt_hi[:, cols], xnt_lo[:, cols]))
                    ins.then_inc(g_done, 1)

            def max_scores(t, b, half, k):
                pe.wait_ge(ghi_ready, 4 * half + k + 1)
                if b % 2 == 0 and k < 2:
                    pe.wait_ge(glo_ready, 4 * half + k + 1)
                wait(pe, max_ready, 4 * t + k - 1)
                pe.wait_ge(diag_ready, 2 * t + 2)
                for i in range(2):
                    ins = nc.tensor.matmul(scores_ps[k % 2][:, i * 2 * P:(i + 1) * 2 * P],
                                           g_hi[:, (b // 2) % 2, 2 * k + i, (b % 2) * P:(b % 2 + 1) * P],
                                           flat(diag_hi[:, b % CB, :, :], 3), start=True, stop=True)
                ins.then_inc(smax_done, 1)

            def transpose_max(t, parity):
                pe.wait_ge(max_ready, 4 * t + 4)
                wait(pe, x2_ready, t - 2)
                wait(pe, maxt_ready, t)
                nc.tensor.transpose(small_ps[0:HEADS, 0:P], row_max[:, parity, :], ident[:]).then_inc(maxt_done, 1)

            def scores(t, b, half, k, loads, projections):
                pairs, q = group(k)
                ps = st_ps[k % 2][:]
                if k == 0:
                    pe.wait_ge(maxrow_in[b % 2], 16 * loads)
                    pe.wait_ge(glo_ready, 4 * half + 4)
                wait(pe, exp_ready, 4 * t + k - 1)
                if projections is not None and k < 2:
                    pe.wait_ge(glo_ready, 4 * projections + k - 1)
                cols = slice((b % 2) * P, (b % 2 + 1) * P)
                split_product(ps, (diag_hi[:, b, q, :], diag_lo[:, b, q, :]),
                              (g_hi[:, b // 2, pairs, cols], g_lo[:, b // 2, pairs, cols]), stop=False)
                heads = max_row[0:1, b % 2, :, :].rearrange("a (h q) n -> a h q n", q=2)
                nc.tensor.matmul(ps, neg_ones[:], heads[:, pairs, q, :], start=False, stop=True).then_inc(st_done, 1)

            def weigh(t, b, k, loads):
                pe.wait_ge(exp_ready, 4 * t + k + 1)
                wait(pe, norm_ready, 4 * t + k - 1)
                if k == 0:
                    pe.wait_ge(keys_in[b], 16 * loads)
                for i in range(4):
                    ins = nc.tensor.matmul(u_ps[k % 2][:, i * (CD + 1):(i + 1) * (CD + 1)], probs_t[:, k, i, :],
                                           ctx_keys[:, b, :], start=True, stop=True)
                ins.then_inc(u_done, 1)

            def transpose_u(t, parity, r):
                pe.wait_ge(norm_ready, 4 * t + 2 * r + 2)
                wait(pe, ut_ready, 2 * t + r)
                for i in range(4):
                    ins = nc.tensor.transpose(ut_ps[:, i * P:(i + 1) * P],
                                              u_norm[:, parity, 4 * r + i, :, :].rearrange("p q d -> p (q d)"), ident[:])
                ins.then_inc(ut_done, 1)

            def route(c, ps):
                pe.wait_ge(x2t_ready, c + 1)
                for i in range(CB):
                    ins = nc.tensor.matmul(ps[:, i * NE:(i + 1) * NE], x2t[:, i * P:(i + 1) * P], router_w[:],
                                           start=True, stop=True)
                ins.then_inc(logits_done, 1)

            def project_out(t, parity, maxima):
                pe.wait_ge(ut_ready, 2 * t + 2)
                pe.wait_ge(maxt_ready, maxima)
                ps = small_ps[:, D:2 * D]
                for p in range(PAIRS):
                    ins = nc.tensor.matmul(ps, u_t[:, parity, p, :], c_pair[:, p, :], start=p == 0, stop=p == PAIRS - 1)
                ins.then_inc(attn_done, 1)

            def fold(left, right, banks):
                for i in range(2):
                    for j in range(4):
                        p = 4 * i + j
                        ins = nc.tensor.matmul(banks[i][:, j * P:(j + 1) * P], left[:, p, :], right[:, p, :],
                                               start=True, stop=True)
                    ins.then_inc(fold_done, 1)

            def keep_busy(products):
                for _ in range(products):
                    nc.tensor.matmul(small_ps[:], c_pair[:, 0, :], c_pair[:, 0:4, :], start=True, stop=True)

            pe.wait_ge(warm_ready, 1)
            keep_busy(WARM_UP)
            pe.wait_ge(wqk_in, 16 * 3)
            fold(wq_pair, wk_diag, scores_ps)
            pe.wait_ge(const_ready, 6)
            transpose_norm(0, ut_ps)
            keep_busy(GAP_1)
            g_project(0, 0, ((glo_ready, -2), (glo_ready, -2)))
            pe.wait_ge(wvo_in, 16 * 3)
            fold(wv_diag, wo_pair, u_ps)
            for k in range(4):
                max_scores(0, 0, 0, k)
            transpose_max(0, 0)
            g_project(1, 0, ((max_ready, 3), (glo_ready, 3)))
            pe.wait_ge(c_ready, 2)
            pe.wait_ge(maxt_ready, 1)
            keep_busy(GAP_2)
            for k in range(4):
                if k < 2:
                    pe.wait_ge(glo_ready, 4 + k + 1)
                max_scores(1, 1, 0, k)

            def attention(c, first, last):
                for b in range(CB):
                    t = CB * c + b
                    for k in range(4):
                        if k == 2 and not (last and b == CB - 1):
                            transpose_max(t + 1, (b + 1) % 2)
                        if not (last and b >= 2):
                            max_scores(t + 2, b + 2, 2 * c + (b + 2) // 2, k)
                        if k == 0 and not (first and b == 0):
                            weigh(t - 1, (b - 1) % CB, 3, c + 1)
                        projections = {0: 2 * c + 2, 2: None if last else 2 * c + 3}.get(b)
                        scores(t, b, 2 * c + b // 2, k, 2 * c + b // 2 + 1, projections)
                        if b == 1 and k == 3:
                            pe.wait_ge(ut_ready, 2 * t)
                            transpose_norm(c + 1, ut_ps)
                        if k > 0:
                            weigh(t, b, k - 1, c + 1)
                        if last and b == 2 and k == 1:
                            pe.wait_ge(ut_ready, 2 * t - 1)
                            route(0, ut_ps)
                        if last and b == 2 and k == 2:
                            pe.wait_ge(logits_ready, 1)
                        if k == 2 and not (first and b == 0):
                            transpose_u(t - 1, (b - 1) % 2, 1)
                        if k == 3:
                            if not (first and b == 0):
                                project_out(t - 1, (b - 1) % 2, t + 1 if last and b == CB - 1 else t + 2)
                            if b == 1:
                                if last:
                                    pe.wait_ge(x2t_ready, 1)
                                else:
                                    pe.wait_ge(xlo_ready, c + 2)
                            transpose_u(t, b % 2, 0)
                    if b % 2 == 1 and not last:
                        g_project(b // 2, c + 1, ((max_ready, 4 * (t + 2) + 3), (exp_ready, 4 * t + 3)))

            in_chunks(pe, attention)
            weigh(NB - 1, CB - 1, 3, NCH)
            transpose_u(NB - 1, (NB - 1) % 2, 1)
            pe.wait_ge(x2_ready, NB - 1)
            project_out(NB - 1, (NB - 1) % 2, NB)

            def weight_halves(kind, u):
                cols = slice(kind * FW + u * P, kind * FW + (u + 1) * P)
                return w_hi[:, cols], w_lo[:, cols]

            x2_halves = [(x2t_hi[:, i, :], x2t_lo[:, i, :]) for i in range(2)]

            def transpose_weights(c):
                pe.wait_ge(parts_ready, c + 1)
                pe.wait_ge(x2_ready, NB)
                pe.wait_ge(logits_ready, c + 1)
                if not isinstance(c, int) or c > 1:
                    pe.wait_ge(result_ready, c - 1)
                ps = misc_ps[:].bitcast(BF16)
                for i in range(CB):
                    ins = nc.tensor.transpose(ps[0:3 * NE, i * P:(i + 1) * P],
                                              w_parts[:, i, :, :].rearrange("p a e -> p (a e)"), ident_bf[:])
                ins.then_inc(wt_done, 1)

            def down(c, u):
                n = UNITS * c + u
                pe.wait_ge(hidlo_ready, n + 1)
                if u == 0:
                    wait(pe, yt_ready, c)
                split_product(y_ps[:], weight_halves(2, u), (hid_hi[:, u % SLOTS, :], hid_lo[:, u % SLOTS, :]),
                              start=u == 0, stop=u == UNITS - 1).then_inc(down_done, 1)

            def transpose_y(c):
                pe.wait_ge(yt_ready, c + 1)
                for i in range(CB):
                    ins = nc.tensor.transpose(misc_ps[:, i * P:(i + 1) * P], y_t[:, i * P:(i + 1) * P], ident[:])
                ins.then_inc(y_done, 1)

            def experts_of(c, parity, first, last):
                for u in range(UNITS):
                    n = UNITS * c + u
                    if u == 0:
                        pe.wait_ge(x2lo_ready, c + 1)
                    wait(pe, silu_ready, free_of(2, c, u))
                    split_product(gate_ps[u % 2][:], weight_halves(0, u), x2_halves[parity]).then_inc(gate_done, 1)
                    wait(pe, gated_ready, free_of(2, c, u))
                    split_product(up_ps[u % 2][:], weight_halves(1, u), x2_halves[parity]).then_inc(up_done, 1)
                    if u > 0:
                        if u == 1:
                            pe.wait_ge(wt_ready, c + 1)
                        wait(pe, hid_ready, free_of(2, c, u))
                        nc.tensor.matmul(wbc_ps[u % 2][:], expand[:, u - 1, :], w_parts_t[:, parity, :],
                                         start=True, stop=True).then_inc(wbc_done, 1)
                    if u >= LAG:
                        down(c, u - LAG)
                    elif not first:
                        down(c - 1, UNITS - LAG + u)
                    if u == 0:
                        transpose_weights(c)
                    if u == 1 and not last:
                        pe.wait_ge(wt_ready, c + 1)
                        transpose_norm(NCH + c + 1, misc_ps)
                    if u == 3 and not last:
                        route(c + 1, misc_ps)
                    if u == 5 and not first:
                        if last:
                            pe.wait_ge(wt_ready, c + 1)
                        else:
                            pe.wait_ge(logits_ready, c + 2)
                        transpose_y(c - 1)

            pe.wait_ge(exp_ready, 4 * NB)
            pe.wait_ge(ut_ready, 2 * NB)
            pe.wait_ge(wsplit_ready, NB)
            pe.wait_ge(const_ready, 9)
            in_chunk_pairs(pe, experts_of)
            for u in range(UNITS - LAG, UNITS):
                down(NCH - 1, u)
            transpose_y(NCH - 1)


def kernel(x, ctx_512, g_xattn, g_ffn, L0_xattn_Wq, L0_xattn_Wk, L0_xattn_Wv, L0_xattn_Wo, L0_xattn_bo,
           L0_ffn_gate_w, L0_ffn_gate_bias, L0_ffn_expert_gate, L0_ffn_expert_up, L0_ffn_expert_down,
           L0_ffn_shared_gate, L0_ffn_shared_up, L0_ffn_shared_down):
    import numpy as np
    import concourse.bacc as bacc
    from concourse.bass_utils import run_bass_kernel_spmd

    lay = np.ascontiguousarray
    ctx = np.asarray(ctx_512)

    def up(w, shared):
        return np.concatenate([np.asarray(shared).T, np.asarray(w).reshape(NE * EI, D).T], axis=1)

    down = np.concatenate([np.asarray(L0_ffn_shared_down).T,
                           np.asarray(L0_ffn_expert_down).transpose(0, 2, 1).reshape(NE * EI, D)], axis=0)
    down = down.reshape(UNITS, P, D).transpose(1, 0, 2).reshape(P, FW)
    experts = np.concatenate([up(L0_ffn_expert_gate, L0_ffn_shared_gate), up(L0_ffn_expert_up, L0_ffn_shared_up), down],
                             axis=1)
    arrays = {
        "x": lay(x), "ctx_nat": lay(ctx.transpose(1, 0, 2)), "ctx_t": lay(ctx.reshape(NB * P, CD).T),
        "g_xattn": lay(g_xattn), "g_ffn": lay(g_ffn), "wq_t": lay(np.asarray(L0_xattn_Wq).T),
        "wk_t": lay(np.asarray(L0_xattn_Wk).T), "wv_t": lay(np.asarray(L0_xattn_Wv).T), "wo": lay(L0_xattn_Wo),
        "bo": lay(L0_xattn_bo), "router_t": lay(np.asarray(L0_ffn_gate_w).T), "router_bias": lay(L0_ffn_gate_bias),
        "experts": lay(experts),
    }
    nc = bacc.Bacc("TRN2", target_bir_lowering=False, num_devices=1)
    ins = [nc.dram_tensor(n, a.shape, F32, kind="ExternalInput").ap() for n, a in arrays.items()]
    out = nc.dram_tensor("out", (NB, P, D), F32, kind="ExternalOutput").ap()
    build(nc, *ins, out)
    r = run_bass_kernel_spmd(nc, [arrays], core_ids=[0])
    return r.results[0]["out"]
```
